# Optimizing a Trainium2 kernel written in Bass

```python
import numpy as np
import jax
import jax.numpy as jnp

def _softmax(x, axis=-1):
    return jax.nn.softmax(x, axis=axis)

def _gelu(x):
    return jax.nn.gelu(x, approximate=True)

def _silu(x):
    return jax.nn.silu(x)

def _sigmoid(x):
    return jax.nn.sigmoid(x)

def _layernorm(x, axis=-1, eps=1e-05):
    m = jnp.mean(x, axis=axis, keepdims=True)
    v = jnp.var(x, axis=axis, keepdims=True)
    return (x - m) / jnp.sqrt(v + eps)

def _scatter_add(tgt, idx, src, axis=0):
    return tgt.at[idx].add(src)

def _segment_sum(src, seg, n):
    return jax.ops.segment_sum(src, seg, n)
kernel_name = 'mk_vit_tower_d1_tok_img1024_r4_bba9a9'

def setup_inputs(seed: int=0):
    np.random.seed(seed)
    _w = jnp.asarray

    def _rec_inputs():
        import jax
        import jax.numpy as jnp
        _rk = jax.random.key(seed)
        x = -0.000392918 + 0.999932 * jax.random.normal(jax.random.fold_in(_rk, 1), (32, 256, 256, 1), jnp.float32)
        return x
    x = _rec_inputs()

    def _L0_tok_setup():
        import jax, jax.numpy as jnp
        import numpy as np
        INV_SQRT2 = 0.7071067811865476
        LEVEL = 3

        def _split(x, axis):
            ax = axis % x.ndim
            sl0 = [slice(None)] * x.ndim
            sl0[ax] = slice(0, None, 2)
            sl1 = [slice(None)] * x.ndim
            sl1[ax] = slice(1, None, 2)
            x0, x1 = (x[tuple(sl0)], x[tuple(sl1)])
            return ((x0 + x1) * INV_SQRT2, (x0 - x1) * INV_SQRT2)

        def _merge(lo, hi, axis):
            ax = axis % lo.ndim
            e = (lo + hi) * INV_SQRT2
            o = (lo - hi) * INV_SQRT2
            s = jnp.stack([e, o], axis=ax + 1)
            shape = list(lo.shape)
            shape[ax] *= 2
            return s.reshape(shape)

        def _dwt2(x):
            lo, hi = _split(x, -1)
            a, h = _split(lo, -2)
            v, d = _split(hi, -2)
            return (a, h, v, d)

        def _idwt2(a, h, v, d):
            lo = _merge(a, h, -2)
            hi = _merge(v, d, -2)
            return _merge(lo, hi, -1)
        key = jax.random.key(seed)
        ks = jax.random.split(key, 8)
        B, H, W = (16, 256, 256)
        x = jax.random.normal(ks[0], (B, H, W, 1), dtype=jnp.float32)
        na = H // 8 * (W // 8)
        n2 = H // 4 * (W // 4)
        n1 = H // 2 * (W // 2)
        scale = 0.02
        Wa = jax.random.normal(ks[1], (na, 1), dtype=jnp.float32) * scale
        ba = jnp.zeros((1,), jnp.float32)
        Wd1 = jax.random.normal(ks[2], (3 * na, 3), dtype=jnp.float32) * scale
        bd1 = jnp.zeros((3,), jnp.float32)
        Wd2 = jax.random.normal(ks[3], (3 * n2, 3), dtype=jnp.float32) * scale
        bd2 = jnp.zeros((3,), jnp.float32)
        Wd3 = jax.random.normal(ks[4], (3 * n1, 3), dtype=jnp.float32) * scale
        bd3 = jnp.zeros((3,), jnp.float32)
        return {'x': x, 'Wa': Wa, 'ba': ba, 'Wd1': Wd1, 'bd1': bd1, 'Wd2': Wd2, 'bd2': bd2, 'Wd3': Wd3, 'bd3': bd3}
    _L0_tok_all = _L0_tok_setup()
    _L0_tok_in = {k: v for k, v in _L0_tok_all.items() if k in ('Wa', 'ba', 'Wd1', 'bd1', 'Wd2', 'bd2', 'Wd3', 'bd3')}
    del _L0_tok_all

    def _L0_attn_setup():
        import jax, jax.numpy as jnp
        import numpy as np
        B, T, E, H = (4, 512, 256, 16)
        S = E // H
        key = jax.random.key(seed)
        ks = jax.random.split(key, 4)
        x = jax.random.normal(ks[0], (B, T, E), dtype=jnp.float32)
        Wk = jax.random.normal(ks[1], (E, E), dtype=jnp.float32) * E ** (-0.5)
        Wq = jax.random.normal(ks[2], (E, E), dtype=jnp.float32) * E ** (-0.5)
        Wo = jax.random.normal(ks[3], (E, E), dtype=jnp.float32) * E ** (-0.5)
        bo = jnp.zeros((E,), dtype=jnp.float32)
        return {'x': x, 'Wk': Wk, 'Wq': Wq, 'Wo': Wo, 'bo': bo}
    _L0_attn_all = _L0_attn_setup()
    _L0_attn_in = {k: v for k, v in _L0_attn_all.items() if k in ('Wk', 'Wq', 'Wo', 'bo')}
    del _L0_attn_all

    def _L0_ffn_setup():
        import jax, jax.numpy as jnp
        import numpy as np
        LN_EPS = 0.001
        EPS = 1e-05
        QB = 128.0

        def ste_round(x):
            return x + jax.lax.stop_gradient(jnp.round(x) - x)
        key = jax.random.key(seed)
        k1, k2 = jax.random.split(key)
        x = jax.random.normal(k1, (4, 2048, 256), dtype=jnp.float32)
        weight = jax.random.normal(k2, (256, 256), dtype=jnp.float32) * 0.02
        ln_gamma = jnp.ones((256,), dtype=jnp.float32)
        ln_beta = jnp.zeros((256,), dtype=jnp.float32)
        return {'x': x, 'weight': weight, 'ln_gamma': ln_gamma, 'ln_beta': ln_beta}
    _L0_ffn_all = _L0_ffn_setup()
    _L0_ffn_in = {k: v for k, v in _L0_ffn_all.items() if k in ('weight', 'ln_gamma', 'ln_beta')}
    del _L0_ffn_all
    return {'x': x, 'L0_tok_Wa': _L0_tok_in['Wa'], 'L0_tok_ba': _L0_tok_in['ba'], 'L0_tok_Wd1': _L0_tok_in['Wd1'], 'L0_tok_bd1': _L0_tok_in['bd1'], 'L0_tok_Wd2': _L0_tok_in['Wd2'], 'L0_tok_bd2': _L0_tok_in['bd2'], 'L0_tok_Wd3': _L0_tok_in['Wd3'], 'L0_tok_bd3': _L0_tok_in['bd3'], 'L0_attn_Wk': _L0_attn_in['Wk'], 'L0_attn_Wq': _L0_attn_in['Wq'], 'L0_attn_Wo': _L0_attn_in['Wo'], 'L0_attn_bo': _L0_attn_in['bo'], 'L0_ffn_weight': _L0_ffn_in['weight'], 'L0_ffn_ln_gamma': _L0_ffn_in['ln_gamma'], 'L0_ffn_ln_beta': _L0_ffn_in['ln_beta']}

def reference(x, L0_tok_Wa, L0_tok_ba, L0_tok_Wd1, L0_tok_bd1, L0_tok_Wd2, L0_tok_bd2, L0_tok_Wd3, L0_tok_bd3, L0_attn_Wk, L0_attn_Wq, L0_attn_Wo, L0_attn_bo, L0_ffn_weight, L0_ffn_ln_gamma, L0_ffn_ln_beta):
    import jax
    import jax.numpy as jnp

    def _L0_tok_ref(x, Wa, ba, Wd1, bd1, Wd2, bd2, Wd3, bd3):
        import jax, jax.numpy as jnp
        import numpy as np
        INV_SQRT2 = 0.7071067811865476
        LEVEL = 3

        def _split(x, axis):
            ax = axis % x.ndim
            sl0 = [slice(None)] * x.ndim
            sl0[ax] = slice(0, None, 2)
            sl1 = [slice(None)] * x.ndim
            sl1[ax] = slice(1, None, 2)
            x0, x1 = (x[tuple(sl0)], x[tuple(sl1)])
            return ((x0 + x1) * INV_SQRT2, (x0 - x1) * INV_SQRT2)

        def _merge(lo, hi, axis):
            ax = axis % lo.ndim
            e = (lo + hi) * INV_SQRT2
            o = (lo - hi) * INV_SQRT2
            s = jnp.stack([e, o], axis=ax + 1)
            shape = list(lo.shape)
            shape[ax] *= 2
            return s.reshape(shape)

        def _dwt2(x):
            lo, hi = _split(x, -1)
            a, h = _split(lo, -2)
            v, d = _split(hi, -2)
            return (a, h, v, d)

        def _idwt2(a, h, v, d):
            lo = _merge(a, h, -2)
            hi = _merge(v, d, -2)
            return _merge(lo, hi, -1)
        img = x[..., 0]
        B = img.shape[0]
        details = []
        cur = img
        for _ in range(LEVEL):
            cur, h, v, d = _dwt2(cur)
            details.append((h, v, d))
        aw = jax.nn.sigmoid(cur.reshape(B, -1) @ Wa + ba)
        rec = cur * aw[:, :, None]
        det_params = [(Wd1, bd1), (Wd2, bd2), (Wd3, bd3)]
        for (h, v, d), (Wd, bd) in zip(reversed(details), det_params):
            flat = jnp.stack([h, v, d], axis=1).reshape(B, -1)
            w = jax.nn.softmax(flat @ Wd + bd, axis=-1)
            rec = _idwt2(rec, h * w[:, 0, None, None], v * w[:, 1, None, None], d * w[:, 2, None, None])
        return rec

    def _L0_attn_ref(x, Wk, Wq, Wo, bo):
        import jax, jax.numpy as jnp
        import numpy as np
        B, T, E, H = (4, 512, 256, 16)
        S = E // H
        b, t, e = x.shape
        h, s = (H, E // H)
        scale = e ** (-0.25)
        k = (x @ Wk).reshape(b, t, h, s).transpose(0, 2, 1, 3)
        q = (x @ Wq).reshape(b, t, h, s).transpose(0, 2, 1, 3)
        v = (x @ Wk).reshape(b, t, h, s).transpose(0, 2, 1, 3)
        dot = jnp.einsum('bhqd,bhkd->bhqk', q * scale, k * scale)
        attn = jax.nn.softmax(dot, axis=-1)
        out = jnp.einsum('bhqk,bhkd->bhqd', attn, v)
        out = out.transpose(0, 2, 1, 3).reshape(b, t, e)
        return out @ Wo + bo

    def _L0_ffn_ref(x, weight, ln_gamma, ln_beta):
        import jax, jax.numpy as jnp
        import numpy as np
        LN_EPS = 0.001
        EPS = 1e-05
        QB = 128.0

        def ste_round(x):
            return x + jax.lax.stop_gradient(jnp.round(x) - x)
        mu = jnp.mean(x, axis=-1, keepdims=True)
        var = jnp.var(x, axis=-1, keepdims=True)
        xn = (x - mu) * jax.lax.rsqrt(var + LN_EPS) * ln_gamma + ln_beta
        beta = jnp.mean(jnp.abs(weight))
        w_q = jnp.clip(ste_round(weight / (beta + EPS)), -1.0, 1.0)
        gamma = jnp.max(jnp.abs(xn))
        xq = jnp.clip(xn * QB / gamma, -QB + EPS, QB - EPS)
        y = jnp.einsum('bsd,du->bsu', xq, w_q)
        return y * (gamma * beta / QB)
    h = _L0_tok_ref(x, L0_tok_Wa, L0_tok_ba, L0_tok_Wd1, L0_tok_bd1, L0_tok_Wd2, L0_tok_bd2, L0_tok_Wd3, L0_tok_bd3)
    h = h + _L0_attn_ref(_layernorm(h, axis=-1), L0_attn_Wk, L0_attn_Wq, L0_attn_Wo, L0_attn_bo)
    h = h + _L0_ffn_ref(_layernorm(h, axis=-1), L0_ffn_weight, L0_ffn_ln_gamma, L0_ffn_ln_beta)
    return h

_drawn_inputs = setup_inputs


def setup_inputs(seed=0):
    import zlib

    import numpy as np

    out = dict(_drawn_inputs(seed))
    spreads = {'L0_tok_bd1': (0.0, 0.539),
     'L0_tok_bd2': (0.0, 0.8),
     'L0_tok_bd3': (0.0, 0.702),
     'L0_attn_bo': (0.0, 0.1),
     'L0_ffn_ln_gamma': (1.0, 0.2),
     'L0_ffn_ln_beta': (0.0, 0.1)}
    factors = {}
    for name, (base, spread) in spreads.items():
        noise = np.random.default_rng([zlib.crc32(name.encode()), seed]).standard_normal(out[name].shape)
        drawn = base * np.exp(spread * noise) if base else spread * noise
        out[name] = jnp.asarray(drawn.astype(out[name].dtype))
    for name, factor in factors.items():
        out[name] = (out[name] * factor).astype(out[name].dtype)
    return out
```

```python
import concourse.bass as bass
from concourse import mybir
from contextlib import ExitStack

F32 = mybir.dt.float32
BF16 = mybir.dt.bfloat16
ALU = mybir.AluOpType
ACT = mybir.ActivationFunctionType
AX = mybir.AxisListType

P = 128
NI = 32
T = 256
E = 256
H = 16
D = E // H
GI = 4
NG = NI // GI
IP = P // GI
RP = T // IP
EC = E // P
QC = T // P
HC = H // EC
PARTS = 3
Q_PARTS = (0, 1, 2, 0, 1, 0)
K_PARTS = (0, 0, 0, 1, 1, 2)
KS = len(Q_PARTS) * D
KM = KS + 2
SCALE = (E ** -0.25) ** 2
LN_EPS = 1e-5
FFN_LN_EPS = 1e-3
FFN_EPS = 1e-5
QB = 128.0
CLIP = QB - FFN_EPS
ROUND = 1.5 * 2.0 ** 23
LEVELS = 3
BAND = [(RP >> (l + 1), E >> (l + 1)) for l in range(LEVELS)]

STACK = 16 * 2 * len(Q_PARTS)
MROW = 16 * 2 * 2
H1_IN = 16 * GI * (RP // QC)
MADE = 2 + GI + 2 + 1 + 1 + 2
POOL_STEPS = 46
DVE_STEPS = 37 

NEXT_PIECES = {5: 2, 6: 1, 7: 1, 8: 1, 9: 2, 10: 1, 11: 1, 12: 1, 13: 1, 14: 1, 15: 1}
REST = H - sum(NEXT_PIECES.values())
REST_PIECES = {h: 1 for h in range(REST)}


def build(nc, x, Wa, ba, Wd1, bd1, Wd2, bd2, Wd3, bd3, Wk, Wq, Wo, bo, Wf, ln_g, ln_b, out):
    parts_dram = nc.dram_tensor("parts_scratch", (2, 2, PARTS, EC, P, T), BF16, kind="Internal").ap()
    h2_dram = nc.dram_tensor("h2_scratch", (NI, P, QC * E), F32, kind="Internal").ap()
    x_v = x.rearrange("(g i) (p r) w c -> g (i p) (r w c)", i=GI, r=RP)
    out_v = out.rearrange("b (p c) e -> b p (c e)", c=QC)

    ctx = ExitStack()
    with ctx:
        def sb(name, shape, dt=F32):
            return ctx.enter_context(nc.sbuf_tensor(name, shape, dt))

        def pb(name, shape=(P, 512)):
            return ctx.enter_context(nc.psum_tensor(name, list(shape), F32))

        def sem(name):
            return ctx.enter_context(nc.semaphore(name))

        img = sb("img", [P, RP * E])
        sd = sb("sd", [P, 2, RP * E // 2])
        coef = [sb(f"coef{l}", [P, 4, r, c]) for l, (r, c) in enumerate(BAND)]
        gw = [sb(f"gw{l}", [P, 3, r * c, 3]) for l, (r, c) in enumerate(BAND)]
        gwa = sb("gwa", [P, BAND[2][0] * BAND[2][1]])
        gbias = sb("gbias", [P, 10])
        gpart = sb("gpart", [P, 10])
        glog = sb("glog", [P, 10])
        gmx = sb("gmx", [P, 3])
        gexp = sb("gexp", [P, 10])
        gsum = sb("gsum", [P, 4])
        grec = sb("grec", [P, 4])
        gate = sb("gate", [P, 10])
        h1 = sb("h1", [P, GI, QC, E])
        h1b = sb("h1b", [P, GI, QC, E])
        bn = sb("bn", [P, QC, 6])
        mv1 = sb("mv1", [P, QC, 2])
        ve1 = sb("ve1", [P, QC])
        rstd1 = sb("rstd1", [P, QC])
        xn = sb("xn", [P, 2, QC, E])
        xnT = sb("xnT", [P, EC, T])
        qk = sb("qk", [P, 2, EC, T])
        qkr = sb("qkr", [P, 2, EC, T])
        parts = sb("parts", [P, 2, PARTS, EC, T], BF16)
        qs = [sb(f"qs{b}", [P, H, T], BF16) for b in range(2)]
        ks = [sb(f"ks{b}", [P, H, T], BF16) for b in range(2)]
        vaug = sb("vaug", [P, GI, QC, H, 2 * D])
        negm = sb("negm", [P, 2, QC, H // 2])
        mT = sb("mT", [H // 2, 2, 2, T], BF16)
        prob = sb("prob", [P, 8, QC, T])
        oT = sb("oT", [P, 4, T])
        rden = sb("rden", [P, 2, 2, QC, 4])
        att = sb("att", [P, QC, E])
        attT = sb("attT", [P, EC, T])
        h2 = sb("h2", [P, 2, QC, E])
        mv2 = sb("mv2", [P, QC, 2])
        rs2 = sb("rs2", [P, 5, QC])
        stats = sb("stats", [P, NI, 2, QC])
        z = sb("z", [P, QC, E])
        zmax = sb("zmax", [P, 2])
        wq = sb("wq", [P, EC, E])
        wk = sb("wk", [P, EC, E])
        wo = sb("wo", [P, EC, E])
        wf = sb("wf", [P, EC, E])
        ident = sb("ident", [P, P])
        ones = sb("ones", [P, P])
        blk1 = sb("blk1", [P, P])
        bo_r = sb("bo_r", [P, QC, E])
        lng = sb("lng", [P, QC, E])
        lnb = sb("lnb", [P, QC, E])
        minus_half = sb("minus_half", [P, QC])
        fs = sb("fs", [P, 8])
        zrow = sb("zrow", [1, P])

        zz = [z[:], att[:]]
        xT = [attT[:].rearrange("p c t -> p (c t)"), xnT[:].rearrange("p c t -> p (c t)")]
        oy = [h1[:, b].rearrange("p c e -> p (c e)") for b in range(2)]

        ps_s = [pb(f"ps_s{b}") for b in range(2)]
        ps_m = [pb(f"ps_m{b}") for b in range(2)]
        ps_o = [pb(f"ps_o{b}") for b in range(2)]
        ps_a, ps_b = pb("ps_a"), pb("ps_b")

        consts_in = sem("consts_in")
        x_in = sem("x_in")
        h1_in = sem("h1_in")
        begun = sem("begun")
        made = sem("made")
        dve_seq = sem("dve_seq")
        pool_seq = sem("pool_seq")
        act_seq = sem("act_seq")
        fwd_done = sem("fwd_done")
        gprod = sem("gprod")
        glog_ps = sem("glog_ps")
        glog_ok = sem("glog_ok")
        gexp_ok = sem("gexp_ok")
        gate_ok = sem("gate_ok")
        scaled = sem("scaled")
        rec_ok = sem("rec_ok")
        var1_ok = sem("var1_ok")
        rstd1_ok = sem("rstd1_ok")
        xn_ok = sem("xn_ok")
        bo_ok = sem("bo_ok")
        xnT_ps = sem("xnT_ps")
        xnT_ok = sem("xnT_ok")
        kT_ps = sem("kT_ps")
        kT_ok = sem("kT_ok")
        qT_ps = sem("qT_ps")
        qT_ok = sem("qT_ok")
        hi_ok = sem("hi_ok")
        res_ok = sem("res_ok")
        parts_ok = sem("parts_ok")
        parts_out = sem("parts_out")
        stack_in = [sem(f"stack_in{b}") for b in range(2)]
        v_ps = sem("v_ps")
        v_ok = sem("v_ok")
        msc_ps = sem("msc_ps")
        max_ok = sem("max_ok")
        mT_ps = sem("mT_ps")
        mhi_ok = sem("mhi_ok")
        mlo_ok = sem("mlo_ok")
        mrow_in = [sem(f"mrow_in{b}") for b in range(2)]
        sc_ps = sem("sc_ps")
        exp_ok = sem("exp_ok")
        pv_ps = sem("pv_ps")
        oT_ok = sem("oT_ok")
        o1_ps = sem("o1_ps")
        att_ok = sem("att_ok")
        attT_ps = sem("attT_ps")
        attT_ok = sem("attT_ok")
        proj_ps = sem("proj_ps")
        h2_ok = sem("h2_ok")
        var2_ok = sem("var2_ok")
        rs2_ok = sem("rs2_ok")
        z_ok = sem("z_ok")
        zb_ok = sem("zb_ok")
        zmax_ok = sem("zmax_ok")
        h2_out = sem("h2_out")
        prep_ps = sem("prep_ps")
        prep_ok = sem("prep_ok")
        c_in = [sem(f"c_in{b}") for b in range(2)]
        c_z = sem("c_z")
        c_zg = sem("c_zg")
        c_cl = sem("c_cl")
        c_zb = sem("c_zb")
        c_x = sem("c_x")
        c_t_ps = sem("c_t_ps")
        c_t = sem("c_t")
        c_y_ps = sem("c_y_ps")
        c_y = sem("c_y")
        c_out = [sem(f"c_out{b}") for b in range(2)]

        class Slot:
            def __init__(self, g, k, fixed):
                self.g, self.k, self.fixed = g, k, fixed
                self.s = fixed if fixed is not None else g * GI + k

            def has(self, o):
                return self.fixed is None or 0 <= self.s + o < NI

            def before(self, o, n):
                return self.fixed is None or self.s + o >= n

            def img(self, o):
                return self.s + o

            def ring(self, o, n):
                return (self.k + o) % n

            def pair(self, o):
                return self.g * 2 + (self.k + o) // 2

            def has_group(self, o):
                return self.fixed is None or 0 <= self.g + o < NG

            def group_before(self, o, n):
                return self.fixed is None or self.g + o >= n

        class Slot:
            def __init__(self, g, k, fixed):
                self.g, self.k, self.fixed = g, k, fixed
                self.s = fixed if fixed is not None else g * GI + k

            def has(self, o):
                return self.fixed is None or 0 <= self.s + o < NI

            def before(self, o, n):
                return self.fixed is None or self.s + o >= n

            def img(self, o):
                return self.s + o

            def ring(self, o, n):
                return (self.k + o) % n

            def pair(self, o):
                return self.g * 2 + (self.k + o) // 2

            def has_group(self, o):
                return self.fixed is None or 0 <= self.g + o < NG

            def group_before(self, o, n):
                return self.fixed is None or self.g + o >= n

        def wait_alone(eng, *waits):
            wait_all(eng, (begun, 1), *waits)

        def wait_all(eng, *waits):
            for _, value in waits:
                eng.compute_val(value)
            for sem, value in waits:
                eng.wait_ge(sem, value)

        class Seq:
            def __init__(self, eng, sem, per_group):
                self.eng, self.sem, self.per_group, self.base, self.n = eng, sem, per_group, 0, 0

            def link(self, ins):
                ins.then_inc(self.sem, 1)
                self.n += 1
                self.eng.wait_ge(self.sem, self.base + self.n)

            def link_alone(self, ins):
                ins.then_inc(self.sem, 1)
                self.n += 1
                wait_alone(self.eng, (self.sem, self.base + self.n))

        FIRST_SLOT = 1 - 2 * GI
        LOOP = (1, NG - 2)

        def run(eng, slot, seq=None):
            for s in range(FIRST_SLOT, LOOP[0] * GI):
                slot(Slot(s // GI, s % GI, s))
            done = seq.n if seq else 0
            with eng.Fori(*LOOP) as g:
                if seq:
                    seq.n, seq.base = 0, (g - LOOP[0]) * seq.per_group + done
                for k in range(GI):
                    slot(Slot(g, k, None))
                if seq:
                    assert seq.n == seq.per_group, f"{seq.n} steps a group, not {seq.per_group}"
            if seq:
                seq.base, seq.n = 0, done + (LOOP[1] - LOOP[0]) * seq.per_group
            for s in range(LOOP[1] * GI, NI + 2):
                slot(Slot(s // GI, s % GI, s))

        block = ctx.enter_context(nc.Block())

        NCONST = 4 + 3 * QC + GI * 4 + 4

        @block.sync
        def _(sp):
            sp.dma_start(img[:], x_v[0]).then_inc(x_in, 16)
            for i in range(GI):
                q = slice(i * IP, (i + 1) * IP)
                for l, w in enumerate((Wd3, Wd2, Wd1)):
                    sp.dma_start(gw[l][q].rearrange("p b f o -> p b (f o)"),
                                 w.rearrange("(b p f) o -> p b (f o)", b=3, p=IP)).then_inc(consts_in, 16)
                sp.dma_start(gwa[q], Wa.rearrange("(p f) o -> p (f o)", p=IP)).then_inc(consts_in, 16)
            for j, b in ((0, bd3), (3, bd2), (6, bd1), (9, ba)):
                sp.dma_start(gbias[:, j:j + b.shape[0]], b.partition_broadcast(P)).then_inc(consts_in, 16)
            for tile, w in ((h2[:, 0], Wq), (h2[:, 1], Wk), (wo[:], Wo), (wf[:], Wf)):
                sp.dma_start(tile, w.rearrange("(c p) n -> p c n", p=P)).then_inc(consts_in, 16)
            for row, b in ((bo_r, bo), (lng, ln_g), (lnb, ln_b)):
                for c in range(QC):
                    sp.dma_start(row[:, c], b.partition_broadcast(P)).then_inc(consts_in, 16)

            def max_rows(t, o, half):
                sp.wait_ge(mlo_ok, 2 * t.img(o) + half + 1)
                for part in range(2):
                    sp.dma_start(qs[t.ring(o, 2)][KS + part:KS + part + 1, half * HC:(half + 1) * HC],
                                 mT[:, half, part]).then_inc(mrow_in[t.ring(o, 2)], 16)

            def slot(t):
                if t.has(1):
                    b = t.ring(1, 2)
                    waits = [(parts_out, 32 * (t.img(1) + 1))]
                    if t.before(1, 2):
                        waits += [(sc_ps, H * t.img(0))]
                    wait_all(sp, *waits)
                    for j in range(len(Q_PARTS)):
                        rows = slice(j * D, (j + 1) * D)
                        for side, (stack, part) in enumerate(((qs[b], Q_PARTS[j]), (ks[b], K_PARTS[j]))):
                            sp.dma_start(stack[rows].rearrange("d (f h) t -> d f (h t)", f=EC),
                                         parts_dram[b, side, part].rearrange("f (d h) t -> d f (h t)", d=D)
                                         ).then_inc(stack_in[b], 16)
                if t.has(0):
                    max_rows(t, 0, 1)
                if t.has(2):
                    b = t.ring(2, 2)
                    waits = [(parts_ok, t.img(2) + 1)]
                    if t.before(2, 2):
                        waits += [(stack_in[b], STACK * (t.pair(0) + 1))]
                    wait_all(sp, *waits)
                    for side in range(2):
                        sp.dma_start(parts_dram[b, side].rearrange("a f p t -> p (a f) t"),
                                     parts[:, side].rearrange("p a f t -> p (a f) t")).then_inc(parts_out, 16)
                if t.has(-1):
                    sp.wait_ge(h2_ok, t.img(0))
                    sp.dma_start(h2_dram[t.img(-1)], h2[:, t.ring(-1, 2)].rearrange("p c e -> p (c e)")
                                 ).then_inc(h2_out, 16)
                if t.has(1):
                    max_rows(t, 1, 0)
                if t.k == 0 and t.has_group(1):
                    waits = [(rec_ok, t.g + 2)]
                    if t.group_before(1, 1):
                        waits += [(xn_ok, t.img(GI)), (bo_ok, t.img(GI))]
                    wait_all(sp, *waits)
                    for i in range(GI):
                        for r in range(RP // QC):
                            sp.dma_start(h1[r::RP // QC, i].rearrange("p c e -> p (c e)"),
                                         img[i * IP:(i + 1) * IP, r * QC * E:(r + 1) * QC * E]
                                         ).then_inc(h1_in, 16)
                    if t.has_group(2):
                        sp.wait_ge(h1_in, H1_IN * (t.g + 2))
                        sp.dma_start(img[:], x_v[t.g + 2]).then_inc(x_in, 16)

            run(sp, slot)

            sp.wait_ge(h2_out, 16 * NI)
            sp.wait_ge(z_ok, NI)

            def load(i, b):
                sp.dma_start(h2[:, b].rearrange("p c e -> p (c e)"), h2_dram[i]).then_inc(c_in[b], 16)

            def store(i, b, n):
                sp.wait_ge(c_y, i + 1)
                sp.dma_start(out_v[i], oy[b]).then_inc(c_out[b], 16)

            load(0, 0)
            load(1, 1)
            with sp.Fori(0, NI // 2 - 1) as n:
                for b in range(2):
                    store(n * 2 + b, b, n)
                    load(n * 2 + b + 2, b)
            for b in range(2):
                store(NI - 2 + b, b, NI // 2 - 1)
            for b in range(2):
                sp.wait_ge(c_out[b], 16 * (NI // 2))

        @block.gpsimd
        def _(pool):
            seq = Seq(pool, pool_seq, POOL_STEPS)
            pool.memset(ident[:], 0.0).then_inc(begun, 1)
            pool.memset(minus_half[:], -0.5).then_inc(made, 1)
            pool.wait_ge(begun, 1)
            pool.affine_select(out=ident[:], in_=ident[:], compare_op=ALU.not_equal, fill=1.0,
                               base=0, pattern=[[-1, P]], channel_multiplier=1).then_inc(made, 1)

            def views(l):
                r, c = BAND[l]
                half = sd[:, :, 0:2 * r * c]
                rows = half.rearrange("p s (r two c) -> p s r two c", two=2, c=c)
                cur = (img[:] if l == 0 else coef[l - 1][:, 0].rearrange("p r c -> p (r c)"))
                return cur.rearrange("p (n two) -> p n two", two=2), half, rows[:, :, :, 0], rows[:, :, :, 1]

            def forward(l):
                cur, half, even, odd = views(l)
                pool.tensor_tensor(half[:, 0], cur[:, :, 0], cur[:, :, 1], ALU.add)
                seq.link(pool.tensor_tensor(half[:, 1], cur[:, :, 0], cur[:, :, 1], ALU.subtract))
                pool.tensor_tensor(coef[l][:, 0::2], even, odd, ALU.add)
                last = pool.tensor_tensor(coef[l][:, 1::2], even, odd, ALU.subtract)
                if l < LEVELS - 1:
                    seq.link_alone(last)
                else:
                    last.then_inc(fwd_done, 1)

            def inverse(l):
                cur, half, even, odd = views(l)
                pool.tensor_tensor(even, coef[l][:, 0::2], coef[l][:, 1::2], ALU.add)
                seq.link(pool.tensor_tensor(odd, coef[l][:, 0::2], coef[l][:, 1::2], ALU.subtract))
                pool.tensor_tensor(cur[:, :, 0], half[:, 0], half[:, 1], ALU.add)
                last = pool.tensor_tensor(cur[:, :, 1], half[:, 0], half[:, 1], ALU.subtract)
                if l:
                    seq.link(last)
                else:
                    last.then_inc(rec_ok, 1)

            def slot(t):
                if t.has(2):
                    waits = [(qT_ok, t.img(2) + 1), (kT_ok, t.img(2) + 1)]
                    if t.before(2, 1):
                        waits += [(parts_out, 32 * t.img(2))]
                    wait_alone(pool, *waits)
                    pool.tensor_copy(parts[:, :, 0], qk[:]).then_inc(hi_ok, 1)
                if t.k == 0 and t.has_group(1):
                    pool.wait_ge(scaled, t.g + 2)
                    for l in reversed(range(LEVELS)):
                        inverse(l)
                if t.k == 1 and t.has_group(2):
                    pool.wait_ge(x_in, 16 * (t.g + 3))
                    forward(0)
                if t.k == 2 and t.has_group(2):
                    forward(1)
                    forward(2)
                if t.has(2):
                    wait_alone(pool, (res_ok, t.img(2) + 1))
                    seq.link(pool.tensor_copy(parts[:, :, 1], qkr[:]))
                    pool.tensor_tensor(parts[:, :, 2], qkr[:], parts[:, :, 1], ALU.subtract).then_inc(parts_ok, 1)
                if t.has(3):
                    wait_alone(pool, (var1_ok, t.img(3) + 1))
                    seq.link(pool.tensor_scalar(ve1[:], mv1[:, :, 1], LN_EPS, None, ALU.add))
                    pool.tensor_tensor(rstd1[:], ve1[:], minus_half[:], ALU.pow).then_inc(rstd1_ok, 1)
                if t.has(-1):
                    waits = [(var2_ok, t.img(0))]
                    if t.before(-1, 1):
                        waits += [(z_ok, t.img(-1))]
                    wait_alone(pool, *waits)
                    var = mv2[:, :, 1]
                    seq.link(pool.tensor_scalar(rs2[:, 0], var, LN_EPS, None, ALU.add))
                    seq.link(pool.tensor_tensor(rs2[:, 1], rs2[:, 0], minus_half[:], ALU.pow))
                    seq.link(pool.tensor_tensor(rs2[:, 2], rs2[:, 1], rs2[:, 1], ALU.mult))
                    seq.link_alone(pool.tensor_tensor(rs2[:, 2], rs2[:, 2], var, ALU.mult))
                    seq.link(pool.tensor_scalar(rs2[:, 2], rs2[:, 2], FFN_LN_EPS, None, ALU.add))
                    seq.link(pool.tensor_tensor(rs2[:, 3], rs2[:, 2], minus_half[:], ALU.pow))
                    pool.tensor_tensor(rs2[:, 4], rs2[:, 1], rs2[:, 3], ALU.mult).then_inc(rs2_ok, 1)
                if t.has(3):
                    if t.before(3, GI):
                        pool.wait_ge(h2_ok, t.img(0))
                    pool.tensor_tensor(h1b[:, t.ring(3, GI)], h1[:, t.ring(3, GI)], bo_r[:], ALU.add).then_inc(bo_ok, 1)
                if t.has(-1):
                    pool.wait_ge(z_ok, t.img(0))
                    seq.link(pool.tensor_tensor(z[:], z[:], lng[:], ALU.mult))
                    pool.tensor_tensor(z[:], z[:], lnb[:], ALU.add).then_inc(zb_ok, 1)

            pool.wait_ge(consts_in, 16 * NCONST)
            run(pool, slot, seq)

            def affine(i, b, n, first):
                pool.wait_ge(c_z, i + 1)
                pool.tensor_tensor(zz[b], zz[b], lng[:], ALU.mult).then_inc(c_zg, 1)
                pool.wait_ge(c_zg, i + 1)
                pool.tensor_tensor(zz[b], zz[b], lnb[:], ALU.add).then_inc(c_zb, 1)
            with pool.Fori(0, NI // 2) as n:
                for b in range(2):
                    affine(n * 2 + b, b, n, False)

        @block.scalar
        def _(act):
            def copy(out, in_, scale=1.0):
                return act.activation(out, in_, ACT.Copy, scale=scale)

            def max_high(t, o, half):
                act.wait_ge(mT_ps, 2 * t.img(o) + half + 1)
                if t.before(o, 1):
                    act.wait_ge(mrow_in[t.ring(o - 1, 2)], MROW * (t.pair(o - 1) + 1))
                copy(mT[:, half, 0], ps_b[0:HC, 0:T]).then_inc(mhi_ok, 1)

            def evac_oT(t, o, bank):
                act.wait_ge(pv_ps, 4 * t.img(o) + 2 * bank + 2)
                if t.before(o, 1):
                    act.wait_ge(o1_ps, 2 * t.img(o - 1) + bank + 1)
                copy(oT[:, 2 * bank:2 * bank + 2].rearrange("p q t -> p (q t)"), ps_o[bank][:]).then_inc(oT_ok, 1)

            def slot(t):
                for h in range(H):
                    if t.has(0):
                        act.wait_ge(sc_ps, H * t.img(0) + h + 1)
                        if h >= 8 or t.before(0, 1):
                            act.wait_ge(pv_ps, 4 * t.img(0) + h // 4 - 1)
                        act.activation(prob[:, h % 8].rearrange("p c t -> p (c t)"), ps_s[h % 2][:],
                                       ACT.Exp).then_inc(exp_ok, 1)
                    if h == 1 and t.has(2):
                        act.wait_ge(xnT_ps, t.img(2) + 1)
                        if t.before(2, 1):
                            act.wait_ge(qT_ps, t.img(2))
                        copy(xnT[:].rearrange("p c t -> p (c t)"), ps_a[:]).then_inc(xnT_ok, 1)
                    if h == 2 and t.has(-1):
                        evac_oT(t, -1, 1)
                    if h == 3 and t.has(2):
                        act.wait_ge(kT_ps, t.img(2) + 1)
                        if t.before(2, 1):
                            act.wait_ge(res_ok, t.img(2))
                            act.wait_ge(v_ps, t.img(2))
                        copy(qk[:, 1].rearrange("p c t -> p (c t)"), ps_b[:]).then_inc(kT_ok, 1)
                    if h == 4 and t.has(2):
                        act.wait_ge(qT_ps, t.img(2) + 1)
                        copy(qk[:, 0].rearrange("p c t -> p (c t)"), ps_a[:], SCALE).then_inc(qT_ok, 1)
                    if h == 5 and t.has(0):
                        max_high(t, 0, 1)
                    if h == 9 and t.has(2):
                        act.wait_ge(v_ps, t.img(2) + 1)
                        if t.before(2, GI):
                            act.wait_ge(pv_ps, 4 * t.img(-1))
                        for c in range(QC):
                            last = copy(vaug[:, t.ring(2, GI), c, :, 0:D].rearrange("p (f h) d -> p f h d", f=EC),
                                        ps_a[:, c * E:(c + 1) * E].rearrange("p (f d h) -> p f h d", f=EC, d=D))
                        last.then_inc(v_ok, 1)
                    if h == 10 and t.has(0):
                        evac_oT(t, 0, 0)
                    if h == 11 and t.has(-1):
                        act.wait_ge(attT_ps, t.img(0))
                        if t.before(-1, 1):
                            act.wait_ge(proj_ps, t.img(-1))
                        copy(attT[:].rearrange("p c t -> p (c t)"), ps_b[:]).then_inc(attT_ok, 1)
                    if h == 15 and t.has(1):
                        max_high(t, 1, 0)
                    if h == 14 and t.k == 3 and t.has_group(2):
                        act.wait_ge(glog_ok, t.g + 3)
                        act.activation(gexp[:], glog[:], ACT.Exp).then_inc(gexp_ok, 1)
                    if h == 2 and t.k == 0 and t.has_group(1):
                        act.wait_ge(gate_ok, t.g + 2)
                        for l in range(LEVELS):
                            for band in range(3):
                                copy(coef[l][:, 1 + band], coef[l][:, 1 + band], gate[:, 3 * l + band:3 * l + band + 1])
                        copy(coef[2][:, 0], coef[2][:, 0], gate[:, 9:10]).then_inc(scaled, 1)

            run(act, slot)

            def second(i, b, n, first):
                act.wait_ge(c_t_ps, i + 1)
                if not first:
                    act.wait_ge(c_y_ps, i - 1)
                copy(xT[b], ps_s[b][:]).then_inc(c_t, 1)
            for b in range(2):
                second(b, b, 0, True)
            with act.Fori(1, NI // 2) as n:
                for b in range(2):
                    second(n * 2 + b, b, n, False)

        @block.vector
        def _(dve):
            seq = Seq(dve, dve_seq, DVE_STEPS)
            link = seq.link
            dve.memset(ones[:], 1.0).then_inc(made, 1)
            link(dve.memset(blk1[:], 0.0))
            for i in range(GI):
                dve.memset(blk1[i * IP:(i + 1) * IP, i * IP:(i + 1) * IP], 1.0).then_inc(made, 1)
            for b in range(2):
                dve.memset(ks[b][KS:P], 1.0).then_inc(made, 1)
            dve.memset(vaug[:], 1.0).then_inc(made, 1)
            link(dve.memset(zmax[:], 0.0))
            dve.wait_ge(consts_in, 16 * NCONST)

            def ternary():
                link(dve.tensor_reduce(fs[:, 0:1], wf[:].rearrange("p c n -> p (c n)"), AX.X, ALU.add,
                                       apply_absolute_value=True))
                dve.wait_ge(made, MADE)
                dve.nop().then_inc(prep_ok, 1)
                dve.wait_ge(prep_ps, 1)
                link(dve.tensor_scalar(fs[:, 1:2], ps_a[:, 0:1], 1.0 / (E * E), None, ALU.mult))
                link(dve.tensor_scalar(fs[:, 2:3], fs[:, 1:2], FFN_EPS, None, ALU.add))
                link(dve.reciprocal(fs[:, 3:4], fs[:, 2:3]))
                link(dve.tensor_scalar(wf[:], wf[:], fs[:, 3:4], 1.0, ALU.mult, ALU.min))
                link(dve.tensor_scalar(wf[:], wf[:], -1.0, ROUND, ALU.max, ALU.add))
                link(dve.tensor_scalar(wf[:], wf[:], -ROUND, None, ALU.add))

            def gate_product(n):
                if n < 3 * LEVELS:
                    l, o = divmod(n, 3)
                    r, c = BAND[l]
                    data = coef[l][:, 1:4].rearrange("p b r c -> p (b r c)")
                    w = gw[l][:].rearrange("p b f o -> p (b f) o")[:, :, o]
                else:
                    r, c = BAND[LEVELS - 1]
                    data, w = coef[LEVELS - 1][:, 0].rearrange("p r c -> p (r c)"), gwa[:]
                size = data.shape[1]
                junk = sd[:].rearrange("p s n -> p (s n)")[:, 0:size]
                return dve.tensor_tensor_reduce(out=junk, in0=data, in1=w, scale=1.0, scalar=0.0,
                                                op0=ALU.mult, op1=ALU.add, accum_out=gpart[:, n:n + 1])

            def gate_logits():
                for l in range(LEVELS):
                    q = slice(3 * l, 3 * l + 3 + (l == LEVELS - 1))
                    last = dve.scalar_tensor_tensor(glog[:, q], ps_a[:, q], 0.5 ** (l + 1), gbias[:, q],
                                                    ALU.mult, ALU.add)
                link(last)
                v = glog[:, 0:9].rearrange("p (l b) -> p l b", b=3)
                link(dve.tensor_reduce(gmx[:], v, AX.X, ALU.max))
                dve.tensor_tensor(v, v, gmx[:].unsqueeze(2).to_broadcast([P, 3, 3]), ALU.subtract)
                dve.tensor_scalar(glog[:, 9:10], glog[:, 9:10], -1.0, None, ALU.mult).then_inc(glog_ok, 1)

            def gate_values(g3):
                dve.wait_ge(gexp_ok, g3)
                v = gexp[:, 0:9].rearrange("p (l b) -> p l b", b=3)
                dve.tensor_reduce(gsum[:, 0:3], v, AX.X, ALU.add)
                link(dve.tensor_scalar(gsum[:, 3:4], gexp[:, 9:10], 1.0, None, ALU.add))
                link(dve.reciprocal(grec[:], gsum[:]))
                for l in range(LEVELS):
                    dve.tensor_scalar(gate[:, 3 * l:3 * l + 3], gexp[:, 3 * l:3 * l + 3], grec[:, l:l + 1],
                                      0.25 ** (l + 1), ALU.mult, ALU.mult)
                dve.tensor_scalar(gate[:, 9:10], grec[:, 3:4], 0.25 ** LEVELS, None, ALU.mult).then_inc(gate_ok, 1)

            def max_low(t, o, half):
                dve.wait_ge(mhi_ok, 2 * t.img(o) + half + 1)
                dve.tensor_tensor(mT[:, half, 1], ps_b[0:HC, 0:T], mT[:, half, 0], ALU.subtract).then_inc(mlo_ok, 1)

            def piece(t, o, n):
                pair, c = divmod(n, QC)
                half, j = divmod(pair, 4)
                dve.wait_ge(msc_ps, H * t.img(o) + n + 1)
                if n % 8 == 0 and t.before(o, 1):
                    dve.wait_ge(mT_ps, 2 * t.img(o - 1) + half + 1)
                dve.tensor_reduce(negm[:, half, c, 2 * j:2 * j + 2], ps_m[n % 2][:].rearrange("p (j t) -> p j t", j=2),
                                  AX.X, ALU.max, negate=True).then_inc(max_ok, 1)

            def normalise(t, bank, ps):
                v = ps[:].rearrange("p (qc j w) -> p qc j w", j=4, w=2 * D)
                dve.wait_ge(o1_ps, 2 * t.img(-1) + bank + 1)
                link(dve.reciprocal(rden[:, bank].rearrange("p q c j -> p (q c) j"), v[:, :, :, D]))
                if bank == 0 and t.before(-1, 1):
                    dve.wait_ge(attT_ps, t.img(-1))
                v5 = v.rearrange("p (q c) j w -> p q c j w", c=QC)
                for c in range(QC):
                    last = dve.tensor_tensor(
                        att[:, c, bank * P:(bank + 1) * P].rearrange("p (q j d) -> p q j d", q=2, j=4),
                        v5[:, :, c, :, 0:D], rden[:, bank, :, c].unsqueeze(3).to_broadcast([P, 2, 4, D]), ALU.mult)
                last.then_inc(att_ok, 1)

            def slot(t):
                done = 0
                for h in range(H):
                    if h in REST_PIECES and t.has(0):
                        piece(t, 0, H - REST + h)
                    if h == 2 and t.has(-2):
                        dve.wait_ge(zb_ok, t.img(-1))
                        link(dve.tensor_reduce(zmax[:, 1:2], z[:].rearrange("p c e -> p (c e)"), AX.X, ALU.max,
                                               apply_absolute_value=True))
                        link(dve.tensor_tensor(zmax[:, 0:1], zmax[:, 0:1], zmax[:, 1:2], ALU.max))
                    if h == 5 and t.has(0):
                        max_low(t, 0, 1)
                    if t.has(1):
                        for _ in range(NEXT_PIECES.get(h, 0)):
                            piece(t, 1, done)
                            done += 1
                    if t.k == 3 and h < 10 and t.has_group(2):
                        if h == 0:
                            dve.wait_ge(fwd_done, t.g + 3)
                        if h == 9:
                            gate_product(h).then_inc(gprod, 1)
                        else:
                            link(gate_product(h))
                    if h == 6 and t.has(-1):
                        normalise(t, 0, ps_a)
                    if h == 7 and t.has(-1):
                        normalise(t, 1, ps_b)
                    if h == 8 and t.has(2):
                        dve.wait_ge(hi_ok, t.img(2) + 1)
                        if t.before(2, 1):
                            dve.wait_ge(parts_ok, t.img(2))
                        dve.tensor_tensor(qkr[:], qk[:], parts[:, :, 0], ALU.subtract).then_inc(res_ok, 1)
                    if h == 10 and t.has(3):
                        if t.ring(3, GI) == 0:
                            dve.wait_ge(h1_in, H1_IN * ((t.g + (t.k + 3) // GI) + 1))
                        for c in range(QC):
                            last = dve.bn_stats(bn[:, c], h1[:, t.ring(3, GI), c])
                        if t.before(3, 1):
                            dve.wait_ge(rstd1_ok, t.img(3))
                        seq.link_alone(last)
                        for c in range(QC):
                            last = dve.bn_aggr(mv1[:, c], bn[:, c])
                        last.then_inc(var1_ok, 1)
                    if h == 12 and t.has(3):
                        dve.wait_ge(rstd1_ok, t.img(3) + 1)
                        if t.before(3, 2):
                            dve.wait_ge(xnT_ps, t.img(2))
                        for c in range(QC):
                            last = dve.tensor_scalar(xn[:, t.ring(3, 2), c], h1[:, t.ring(3, GI), c],
                                                     mv1[:, c, 0:1], rstd1[:, c:c + 1], ALU.subtract, ALU.mult)
                        last.then_inc(xn_ok, 1)
                    if h == 13 and t.has(-1):
                        b = t.ring(-1, 2)
                        dve.wait_ge(proj_ps, t.img(0))
                        dve.wait_ge(bo_ok, t.img(0))
                        if t.before(-1, 2):
                            dve.wait_ge(h2_out, 16 * t.img(-1))
                        dve.tensor_tensor(h2[:, b].rearrange("p c e -> p (c e)"), ps_a[:],
                                          h1b[:, t.ring(-1, GI)].rearrange("p c e -> p (c e)"), ALU.add).then_inc(h2_ok, 1)
                        dve.wait_ge(h2_ok, t.img(0))
                        for c in range(QC):
                            last = dve.bn_stats(bn[:, c], h2[:, b, c])
                        if t.before(-1, 1):
                            dve.wait_ge(rs2_ok, t.img(-1))
                        seq.link_alone(last)
                        for c in range(QC):
                            last = dve.bn_aggr(mv2[:, c], bn[:, c])
                        last.then_inc(var2_ok, 1)
                    if h == 14 and t.k == 3 and t.has_group(2):
                        dve.wait_ge(glog_ps, t.g + 3)
                        gate_logits()
                    if h == 15 and t.has(1):
                        max_low(t, 1, 0)
                    if h == 15 and t.k == 3 and t.has_group(2):
                        gate_values(t.g + 3)
                    if h == 15 and t.has(-1):
                        dve.wait_ge(rs2_ok, t.img(0))
                        for c in range(QC):
                            last = dve.tensor_scalar(z[:, c], h2[:, t.ring(-1, 2), c], mv2[:, c, 0:1],
                                                     rs2[:, 4, c:c + 1], ALU.subtract, ALU.mult)
                        dve.tensor_copy(stats[:, t.img(-1), 0], mv2[:, :, 0])
                        dve.tensor_copy(stats[:, t.img(-1), 1], rs2[:, 4]).then_inc(z_ok, 1)

            for side, w in enumerate((wq, wk)):
                dve.tensor_copy(w[:].rearrange("p e (f d h) -> p (e f) d h", f=EC, d=D),
                                h2[:, side].rearrange("p e (f h d) -> p (e f) d h", f=EC, d=D)).then_inc(made, 1)
            ternary()
            run(dve, slot, seq)

            dve.nop().then_inc(prep_ok, 1)
            dve.wait_ge(prep_ps, 2)
            link(dve.tensor_reduce(zrow[:, 0:1], ps_a[0:1, 0:P], AX.X, ALU.max))
            dve.nop().then_inc(prep_ok, 1)
            dve.wait_ge(prep_ps, 3)
            link(dve.tensor_scalar(fs[:, 4:5], ps_b[:, 0:1], 1.0, None, ALU.mult))
            link(dve.reciprocal(fs[:, 5:6], fs[:, 4:5]))
            link(dve.tensor_scalar(fs[:, 5:6], fs[:, 5:6], QB, None, ALU.mult))
            link(dve.tensor_scalar(fs[:, 6:7], fs[:, 4:5], fs[:, 1:2], 1.0 / QB, ALU.mult, ALU.mult))

            def normed(i, b, n, first):
                dve.wait_ge(c_in[b], 16 * (n + 1))
                if not first:
                    dve.wait_ge(c_t_ps, i - 1)
                for c in range(QC):
                    last = dve.tensor_scalar(zz[b][:, c], h2[:, b, c], stats[:, i, 0, c:c + 1],
                                             stats[:, i, 1, c:c + 1], ALU.subtract, ALU.mult)
                last.then_inc(c_z, 1)

            def clipped(i, b, n, first):
                dve.wait_ge(c_zb, i + 1)
                dve.tensor_scalar(zz[b], zz[b], fs[:, 5:6], CLIP, ALU.mult, ALU.min).then_inc(c_cl, 1)
                dve.wait_ge(c_cl, i + 1)
                dve.tensor_scalar(zz[b], zz[b], -CLIP, None, ALU.max).then_inc(c_x, 1)

            def summed(i, b, n, first):
                dve.wait_ge(c_y_ps, i + 1)
                if not first:
                    dve.wait_ge(c_out[b], 16 * n)
                dve.scalar_tensor_tensor(oy[b], ps_m[b][:], fs[:, 6:7], h2[:, b].rearrange("p c e -> p (c e)"),
                                         ALU.mult, ALU.add).then_inc(c_y, 1)

            def pair(n, first):
                normed(n * 2, 0, n, first)
                if not first:
                    summed(n * 2 - 1, 1, n - 1, isinstance(n, int))
                clipped(n * 2, 0, n, first)
                normed(n * 2 + 1, 1, n, first)
                summed(n * 2, 0, n, first)
                clipped(n * 2 + 1, 1, n, first)
            pair(0, True)
            pair(1, False)
            with dve.Fori(2, NI // 2) as n:
                pair(n, False)
            summed(NI - 1, 1, NI // 2 - 1, False)

        @block.tensor
        def _(pe):
            def transposes(t, ps, tile):
                for e in range(2):
                    for c in range(2):
                        last = pe.transpose(ps[:, e * T + c * P:e * T + (c + 1) * P], tile[:, c, e * P:(e + 1) * P],
                                            ident[:])
                return last

            def project(ps, w):
                for f in range(EC):
                    for e in range(EC):
                        last = pe.matmul(ps[:, f * T:(f + 1) * T],
                                         w[:, e, f * P:(f + 1) * P], xnT[:, e], start=(e == 0), stop=(e == EC - 1))
                return last

            def maxima_rows(t, o, half):
                pe.wait_ge(max_ok, H * t.img(o) + 8 * (half + 1))
                for c in range(QC):
                    last = pe.transpose(ps_b[0:HC, c * P:(c + 1) * P], negm[:, half, c], ident[:])
                last.then_inc(mT_ps, 1)

            def piece(t, o, n):
                pair, c = divmod(n, QC)
                if n == 0:
                    pe.wait_ge(stack_in[t.ring(o, 2)], STACK * (t.pair(o) + 1))
                if n >= 2 or t.before(o, 1):
                    pe.wait_ge(max_ok, H * t.img(o) + n - 1)
                for j in range(2):
                    q = qs[t.ring(o, 2)][0:KS, 2 * pair + j, c * P:(c + 1) * P]
                    last = pe.matmul(ps_m[n % 2][:, j * T:(j + 1) * T], q, ks[t.ring(o, 2)][0:KS, 2 * pair + j],
                                     start=True, stop=True)
                last.then_inc(msc_ps, 1)

            def values(t, o, quad):
                if quad == 0:
                    pe.wait_ge(v_ok, t.img(o) + 1)
                pe.wait_ge(exp_ok, H * t.img(o) + 4 * (quad + 1))
                if quad % 2 == 0 and t.before(o, 1):
                    pe.wait_ge(oT_ok, 2 * t.img(o - 1) + quad // 2 + 1)
                for c in range(QC):
                    for j in range(4):
                        last = pe.matmul(ps_o[quad // 2][j * 2 * D:(j + 1) * 2 * D, (quad % 2) * T:(quad % 2 + 1) * T],
                                         vaug[:, t.ring(o, GI), c, 4 * quad + j], prob[:, (4 * quad + j) % 8, c],
                                         start=(c == 0), stop=(c == QC - 1))
                last.then_inc(pv_ps, 1)

            def tokens(t, bank, ps):
                pe.wait_ge(oT_ok, 2 * t.img(-1) + bank + 1)
                for q in range(2):
                    for c in range(QC):
                        last = pe.transpose(ps[:, (q * QC + c) * P:(q * QC + c + 1) * P],
                                            oT[:, 2 * bank + q, c * P:(c + 1) * P], ident[:])
                last.then_inc(o1_ps, 1)

            def slot(t):
                done = 0
                for h in range(H):
                    if t.has(0):
                        if h % HC == 0:
                            pe.wait_ge(mrow_in[t.ring(0, 2)], MROW * t.pair(0) + 32 * (h // HC + 1))
                        if h >= 2 or t.before(0, 1):
                            pe.wait_ge(exp_ok, H * t.img(0) + h - 1)
                        for c in range(QC):
                            last = pe.matmul(ps_s[h % 2][:, c * T:(c + 1) * T],
                                             ks[t.ring(0, 2)][0:KM, h, c * P:(c + 1) * P], qs[t.ring(0, 2)][0:KM, h],
                                             start=True, stop=True)
                        last.then_inc(sc_ps, 1)
                    if h in REST_PIECES and t.has(0):
                        piece(t, 0, H - REST + h)
                    if h == 1 and t.has(-1):
                        values(t, -1, 3)
                    if h in (5, 9, 13) and t.has(0):
                        values(t, 0, (h - 5) // 4)
                    if h == 0 and t.has(2):
                        if t.has(-2):
                            pe.wait_ge(h2_ok, t.img(-1))
                        elif t.has(1):
                            pe.wait_ge(v_ok, t.img(2))
                        if t.k == 0 and t.has_group(1):
                            pe.wait_ge(glog_ok, t.g + 2)
                        pe.wait_ge(xn_ok, t.img(2) + 1)
                        transposes(t, ps_a, xn[:, t.ring(2, 2)]).then_inc(xnT_ps, 1)
                    if h == 2 and t.has(2):
                        if t.has(0):
                            pe.wait_ge(mlo_ok, 2 * t.img(0) + 1)
                        pe.wait_ge(xnT_ok, t.img(2) + 1)
                        project(ps_b, wk).then_inc(kT_ps, 1)
                    if h == 3 and t.has(2):
                        project(ps_a, wq).then_inc(qT_ps, 1)
                    if h == 4 and t.has(0):
                        if t.has(2):
                            pe.wait_ge(kT_ok, t.img(2) + 1)
                        else:
                            pe.wait_ge(mlo_ok, 2 * t.img(0) + 1)
                        maxima_rows(t, 0, 1)
                    if h == 5 and t.has(-1):
                        if t.has(2):
                            pe.wait_ge(qT_ok, t.img(2) + 1)
                        elif t.has(-2):
                            pe.wait_ge(h2_ok, t.img(-1))
                        tokens(t, 0, ps_a)
                    if h == 6 and t.has(-1):
                        if t.has(0):
                            pe.wait_ge(mlo_ok, 2 * t.img(0) + 2)
                        else:
                            pe.wait_ge(attT_ok, t.img(-1))
                        tokens(t, 1, ps_b)
                    if h == 8 and t.has(2):
                        if t.has(-1):
                            pe.wait_ge(att_ok, 2 * t.img(-1) + 1)
                        pe.wait_ge(kT_ok, t.img(2) + 1)
                        pe.wait_ge(qT_ok, t.img(2) + 1)
                        transposes_kT(t)
                    if h == 9 and t.has(-1):
                        pe.wait_ge(att_ok, 2 * t.img(0))
                        transposes(t, ps_b, att).then_inc(attT_ps, 1)
                    if h == 11 and t.has(-1):
                        pe.wait_ge(attT_ok, t.img(0))
                        if t.has(2):
                            pe.wait_ge(v_ok, t.img(2) + 1)
                        for c in range(QC):
                            for e in range(EC):
                                last = pe.matmul(ps_a[:, c * E:(c + 1) * E], attT[:, e, c * P:(c + 1) * P], wo[:, e],
                                                 start=(e == 0), stop=(e == EC - 1))
                        last.then_inc(proj_ps, 1)
                    if t.has(1):
                        for _ in range(NEXT_PIECES.get(h, 0)):
                            piece(t, 1, done)
                            done += 1
                    if h == 13 and t.k == 3 and t.has_group(2):
                        pe.wait_ge(gprod, t.g + 3)
                        if t.has(-1):
                            pe.wait_ge(h2_ok, t.img(0))
                        elif t.has(2):
                            pe.wait_ge(v_ok, t.img(2) + 1)
                        pe.matmul(ps_a[:, 0:10], blk1[:], gpart[:], start=True, stop=True).then_inc(glog_ps, 1)
                    if h == 14 and t.has(1):
                        if t.has(-1):
                            pe.wait_ge(attT_ok, t.img(0))
                        elif t.has(0):
                            pe.wait_ge(mlo_ok, 2 * t.img(0) + 2)
                        elif t.has(2):
                            pe.wait_ge(kT_ok, t.img(2) + 1)
                        maxima_rows(t, 1, 0)

            def transposes_kT(t):
                for c in range(QC):
                    for f in range(EC):
                        last = pe.transpose(ps_a[:, (c * EC + f) * P:(c * EC + f + 1) * P],
                                            qk[:, 1, f, c * P:(c + 1) * P], ident[:])
                last.then_inc(v_ps, 1)

            pe.wait_ge(made, MADE)
            pe.wait_ge(consts_in, 16 * NCONST)
            pe.wait_ge(prep_ok, 1)
            pe.matmul(ps_a[:, 0:1], ones[:], fs[:, 0:1], start=True, stop=True).then_inc(prep_ps, 1)
            pe.wait_ge(dve_seq, 4)
            run(pe, slot)
            pe.wait_ge(prep_ok, 2)
            pe.transpose(ps_a[0:1, 0:P], zmax[:, 0:1], ident[:]).then_inc(prep_ps, 1)
            pe.wait_ge(prep_ok, 3)
            pe.matmul(ps_b[:, 0:1], ones[0:1, :], zrow[:, 0:1], start=True, stop=True).then_inc(prep_ps, 1)

            def turned(i, b, n, first):
                pe.wait_ge(c_x, i + 1)
                if not first:
                    pe.wait_ge(c_t, i - 1)
                transposes(None, ps_s[b], zz[b]).then_inc(c_t_ps, 1)

            def fed(i, b, n, first):
                pe.wait_ge(c_t, i + 1)
                if not first:
                    pe.wait_ge(c_y, i - 1)
                for c in range(QC):
                    for e in range(EC):
                        last = pe.matmul(ps_m[b][:, c * E:(c + 1) * E], xT[b][:, e * T + c * P:e * T + (c + 1) * P],
                                         wf[:, e], start=(e == 0), stop=(e == EC - 1))
                last.then_inc(c_y_ps, 1)

            for b in range(2):
                turned(b, b, 0, True)
                fed(b, b, 0, True)
            with pe.Fori(1, NI // 2) as n:
                for b in range(2):
                    turned(n * 2 + b, b, n, False)
                    fed(n * 2 + b, b, n, False)


_INS = ["x", "L0_tok_Wa", "L0_tok_ba", "L0_tok_Wd1", "L0_tok_bd1", "L0_tok_Wd2", "L0_tok_bd2", "L0_tok_Wd3",
        "L0_tok_bd3", "L0_attn_Wk", "L0_attn_Wq", "L0_attn_Wo", "L0_attn_bo", "L0_ffn_weight", "L0_ffn_ln_gamma",
        "L0_ffn_ln_beta"]


def kernel(**inputs):
    import numpy as np
    import concourse.bacc as bacc
    from concourse.bass_utils import run_bass_kernel_spmd

    nc = bacc.Bacc("TRN2", target_bir_lowering=False, num_devices=1)
    arrays, args = {}, []
    for name in _INS:
        a = np.ascontiguousarray(inputs[name])
        arrays[name] = a
        args.append(nc.dram_tensor(name, a.shape, mybir.dt.from_np(a.dtype), kind="ExternalInput").ap())
    out = nc.dram_tensor("out", (NI, T, E), F32, kind="ExternalOutput").ap()
    build(nc, *args, out)
    return run_bass_kernel_spmd(nc, [arrays], core_ids=[0]).results[0]["out"]
```

```python
import concourse.bass as bass
from concourse import mybir
from contextlib import ExitStack

F32 = mybir.dt.float32
BF16 = mybir.dt.bfloat16
ALU = mybir.AluOpType
ACT = mybir.ActivationFunctionType
AX = mybir.AxisListType

P = 128
NI = 32
T = 256
E = 256
H = 16
D = E // H
GI = 4
NG = NI // GI
IP = P // GI
RP = T // IP
EC = E // P
QC = T // P
HC = H // EC
PARTS = 3
Q_PARTS = (0, 1, 2, 0, 1, 0)
K_PARTS = (0, 0, 0, 1, 1, 2)
KS = len(Q_PARTS) * D
KM = KS + 2
SCALE = (E ** -0.25) ** 2
LN_EPS = 1e-5
FFN_LN_EPS = 1e-3
FFN_EPS = 1e-5
QB = 128.0
CLIP = QB - FFN_EPS
ROUND = 1.5 * 2.0 ** 23
LEVELS = 3
BAND = [(RP >> (l + 1), E >> (l + 1)) for l in range(LEVELS)]

STACK = 16 * 6
MROW = 16 * 2 * 2
H1_IN = 16 * GI * (RP // QC)
MADE = 2 + GI + 2 + 1 + 1 + 2
POOL_STEPS = 49
DVE_STEPS = 37 

HALF = H // 2


def build(nc, x, Wa, ba, Wd1, bd1, Wd2, bd2, Wd3, bd3, Wk, Wq, Wo, bo, Wf, ln_g, ln_b, out):
    parts_dram = nc.dram_tensor("parts_scratch", (2, 2, PARTS, EC, P, T), BF16, kind="Internal").ap()
    h2_dram = nc.dram_tensor("h2_scratch", (NI, P, QC * E), F32, kind="Internal").ap()
    x_v = x.rearrange("(g i) (p r) w c -> g (i p) (r w c)", i=GI, r=RP)
    out_v = out.rearrange("b (p c) e -> b p (c e)", c=QC)

    ctx = ExitStack()
    with ctx:
        def sb(name, shape, dt=F32):
            return ctx.enter_context(nc.sbuf_tensor(name, shape, dt))

        def pb(name, shape=(P, 512)):
            return ctx.enter_context(nc.psum_tensor(name, list(shape), F32))

        def sem(name):
            return ctx.enter_context(nc.semaphore(name))

        img = sb("img", [P, RP * E])
        sd = sb("sd", [P, 2, RP * E // 2])
        coef = [sb(f"coef{l}", [P, 4, r, c]) for l, (r, c) in enumerate(BAND)]
        gw = [sb(f"gw{l}", [P, 3, r * c, 3]) for l, (r, c) in enumerate(BAND)]
        gwa = sb("gwa", [P, BAND[2][0] * BAND[2][1]])
        gbias = sb("gbias", [P, 10])
        gpart = sb("gpart", [P, 10])
        glog = sb("glog", [P, 10])
        gmx = sb("gmx", [P, 3])
        gexp = sb("gexp", [P, 10])
        gsum = sb("gsum", [P, 4])
        grec = sb("grec", [P, 4])
        gate = sb("gate", [P, 10])
        h1 = sb("h1", [P, GI, QC, E])
        h1b = sb("h1b", [P, GI, QC, E])
        bn = sb("bn", [P, QC, 6])
        mv1 = sb("mv1", [P, QC, 2])
        ve1 = sb("ve1", [P, QC])
        rstd1 = sb("rstd1", [P, QC])
        xn = sb("xn", [P, 2, QC, E])
        xnT = sb("xnT", [P, EC, T])
        qk = sb("qk", [P, 2, EC, T])
        qkr = sb("qkr", [P, 2, EC, T])
        parts = sb("parts", [P, 2, PARTS, EC, T], BF16)
        qs = [sb(f"qs{b}", [P, H, T], BF16) for b in range(2)]
        ks = [sb(f"ks{b}", [P, H, T], BF16) for b in range(2)]
        vaug = sb("vaug", [P, GI, QC, H, 2 * D])
        negm = sb("negm", [P, 2, QC, H // 2])
        m32 = sb("m32", [H // 2, 2, T])
        mT = sb("mT", [H // 2, 2, 2, T], BF16)
        prob = sb("prob", [P, 8, QC, T])
        oT = sb("oT", [P, 4, T])
        rden = sb("rden", [P, 2, 2, QC, 4])
        att = sb("att", [P, QC, E])
        attT = sb("attT", [P, EC, T])
        h2 = sb("h2", [P, 2, QC, E])
        mv2 = sb("mv2", [P, QC, 2])
        rs2 = sb("rs2", [P, 5, QC])
        stats = sb("stats", [P, NI, 2, QC])
        z = sb("z", [P, QC, E])
        zmax = sb("zmax", [P, 2])
        wq = sb("wq", [P, EC, E])
        wk = sb("wk", [P, EC, E])
        wo = sb("wo", [P, EC, E])
        wf = sb("wf", [P, EC, E])
        ident = sb("ident", [P, P])
        ones = sb("ones", [P, P])
        blk1 = sb("blk1", [P, P])
        bo_r = sb("bo_r", [P, QC, E])
        lng = sb("lng", [P, QC, E])
        lnb = sb("lnb", [P, QC, E])
        minus_half = sb("minus_half", [P, QC])
        fs = sb("fs", [P, 8])
        zrow = sb("zrow", [1, P])

        hh = [prob[:, b].rearrange("p c e -> p (c e)") for b in range(8)]
        zz = [vaug[:, b].rearrange("p c h d -> p (c h d)")[:, 0:QC * E] for b in range(GI)]
        xT = [attT[:].rearrange("p c t -> p (c t)"), xnT[:].rearrange("p c t -> p (c t)")]
        oy = [h1[:, b].rearrange("p c e -> p (c e)") for b in range(GI)]

        lng_v, lnb_v = (r[:].rearrange("p c e -> p (c e)") for r in (lng, lnb))

        ps_s = [pb(f"ps_s{b}") for b in range(2)]
        ps_m = [pb(f"ps_m{b}") for b in range(2)]
        ps_o = [pb(f"ps_o{b}") for b in range(2)]
        ps_a, ps_b = pb("ps_a"), pb("ps_b")

        consts_in = sem("consts_in")
        x_in = sem("x_in")
        h1_in = sem("h1_in")
        begun = sem("begun")
        made = sem("made")
        dve_seq = sem("dve_seq")
        pool_seq = sem("pool_seq")
        act_seq = sem("act_seq")
        fwd_done = sem("fwd_done")
        gprod = sem("gprod")
        glog_ps = sem("glog_ps")
        glog_ok = sem("glog_ok")
        gexp_ok = sem("gexp_ok")
        gate_ok = sem("gate_ok")
        scaled = sem("scaled")
        rec_ok = sem("rec_ok")
        var1_ok = sem("var1_ok")
        rstd1_ok = sem("rstd1_ok")
        xn_ok = sem("xn_ok")
        bo_ok = sem("bo_ok")
        xnT_ps = sem("xnT_ps")
        xnT_ok = sem("xnT_ok")
        kT_ps = sem("kT_ps")
        kT_ok = sem("kT_ok")
        qT_ps = sem("qT_ps")
        qT_ok = sem("qT_ok")
        res_ok = sem("res_ok")
        mid_ok = sem("mid_ok")
        parts_ok = sem("parts_ok")
        parts_out = sem("parts_out")
        stack_in = [[sem(f"stack_in{b}{f}") for f in range(2)] for b in range(2)]
        v_ps = sem("v_ps")
        v_ok = sem("v_ok")
        msc_ps = sem("msc_ps")
        max_ok = sem("max_ok")
        mT_ps = sem("mT_ps")
        mhi_ok = sem("mhi_ok")
        mlo_ok = sem("mlo_ok")
        mrow_in = [sem(f"mrow_in{b}") for b in range(2)]
        sc_ps = sem("sc_ps")
        exp_ok = sem("exp_ok")
        pv_ps = sem("pv_ps")
        oT_ok = sem("oT_ok")
        o1_ps = sem("o1_ps")
        att_ok = sem("att_ok")
        attT_ps = sem("attT_ps")
        attT_ok = sem("attT_ok")
        proj_ps = sem("proj_ps")
        h2_ok = sem("h2_ok")
        var2_ok = sem("var2_ok")
        rs2_ok = sem("rs2_ok")
        z_ok = sem("z_ok")
        zb_ok = sem("zb_ok")
        zmax_ok = sem("zmax_ok")
        h2_out = sem("h2_out")
        prep_ps = sem("prep_ps")
        prep_ok = sem("prep_ok")
        c_in = [sem(f"c_in{b}") for b in range(8)]
        c_z = sem("c_z")
        c_zg = sem("c_zg")
        c_cl = sem("c_cl")
        c_zb = sem("c_zb")
        c_x = sem("c_x")
        c_t_ps = sem("c_t_ps")
        c_t = sem("c_t")
        c_y_ps = sem("c_y_ps")
        c_y = sem("c_y")
        c_out = [sem(f"c_out{b}") for b in range(4)]

        class Slot:
            def __init__(self, g, k, fixed):
                self.g, self.k, self.fixed = g, k, fixed
                self.s = fixed if fixed is not None else g * GI + k

            def has(self, o):
                return self.fixed is None or 0 <= self.s + o < NI

            def before(self, o, n):
                return self.fixed is None or self.s + o >= n

            def img(self, o):
                return self.s + o

            def ring(self, o, n):
                return (self.k + o) % n

            def pair(self, o):
                return self.g * 2 + (self.k + o) // 2

            def has_group(self, o):
                return self.fixed is None or 0 <= self.g + o < NG

            def group_before(self, o, n):
                return self.fixed is None or self.g + o >= n

        class Slot:
            def __init__(self, g, k, fixed):
                self.g, self.k, self.fixed = g, k, fixed
                self.s = fixed if fixed is not None else g * GI + k

            def has(self, o):
                return self.fixed is None or 0 <= self.s + o < NI

            def before(self, o, n):
                return self.fixed is None or self.s + o >= n

            def img(self, o):
                return self.s + o

            def ring(self, o, n):
                return (self.k + o) % n

            def pair(self, o):
                return self.g * 2 + (self.k + o) // 2

            def has_group(self, o):
                return self.fixed is None or 0 <= self.g + o < NG

            def group_before(self, o, n):
                return self.fixed is None or self.g + o >= n

        def wait_alone(eng, *waits):
            wait_all(eng, (begun, 1), *waits)

        def wait_all(eng, *waits):
            for _, value in waits:
                eng.compute_val(value)
            for sem, value in waits:
                eng.wait_ge(sem, value)

        class Seq:
            def __init__(self, eng, sem, per_group):
                self.eng, self.sem, self.per_group, self.base, self.n = eng, sem, per_group, 0, 0

            def link(self, ins):
                ins.then_inc(self.sem, 1)
                self.n += 1
                self.eng.wait_ge(self.sem, self.base + self.n)

            def link_alone(self, ins):
                ins.then_inc(self.sem, 1)
                self.n += 1
                wait_alone(self.eng, (self.sem, self.base + self.n))

        FIRST_SLOT = 1 - 2 * GI
        LOOP = (1, NG - 2)

        def run(eng, slot, seq=None):
            for s in range(FIRST_SLOT, LOOP[0] * GI):
                slot(Slot(s // GI, s % GI, s))
            done = seq.n if seq else 0
            with eng.Fori(*LOOP) as g:
                if seq:
                    seq.n, seq.base = 0, (g - LOOP[0]) * seq.per_group + done
                for k in range(GI):
                    slot(Slot(g, k, None))
                if seq:
                    assert seq.n == seq.per_group, f"{seq.n} steps a group, not {seq.per_group}"
            if seq:
                seq.base, seq.n = 0, done + (LOOP[1] - LOOP[0]) * seq.per_group
            for s in range(LOOP[1] * GI, NI + 2):
                slot(Slot(s // GI, s % GI, s))

        BODY2 = 8

        def run2(eng, slot):
            for s in range(-4, BODY2):
                slot(Slot2(s // BODY2, s % BODY2, s))
            with eng.Fori(1, NI // BODY2 - 1) as g:
                for k in range(BODY2):
                    slot(Slot2(g, k, None))
            for s in range(NI - BODY2, NI + 2):
                slot(Slot2(s // BODY2, s % BODY2, s))

        class Slot2(Slot):
            def __init__(self, g, k, fixed):
                super().__init__(g, k, fixed)
                self.s = fixed if fixed is not None else g * BODY2 + k

            def turn(self, o, n):
                return self.g * (BODY2 // n) + (self.k + o) // n

        block = ctx.enter_context(nc.Block())

        NCONST = 4 + 3 * QC + GI * 4 + 4

        @block.sync
        def _(sp):
            sp.dma_start(img[:], x_v[0]).then_inc(x_in, 16)
            for i in range(GI):
                q = slice(i * IP, (i + 1) * IP)
                for l, w in enumerate((Wd3, Wd2, Wd1)):
                    sp.dma_start(gw[l][q].rearrange("p b f o -> p b (f o)"),
                                 w.rearrange("(b p f) o -> p b (f o)", b=3, p=IP)).then_inc(consts_in, 16)
                sp.dma_start(gwa[q], Wa.rearrange("(p f) o -> p (f o)", p=IP)).then_inc(consts_in, 16)
            for j, b in ((0, bd3), (3, bd2), (6, bd1), (9, ba)):
                sp.dma_start(gbias[:, j:j + b.shape[0]], b.partition_broadcast(P)).then_inc(consts_in, 16)
            for tile, w in ((h2[:, 0], Wq), (h2[:, 1], Wk), (wo[:], Wo), (wf[:], Wf)):
                sp.dma_start(tile, w.rearrange("(c p) n -> p c n", p=P)).then_inc(consts_in, 16)
            for row, b in ((bo_r, bo), (lng, ln_g), (lnb, ln_b)):
                for c in range(QC):
                    sp.dma_start(row[:, c], b.partition_broadcast(P)).then_inc(consts_in, 16)

            def max_rows(t, o, half):
                sp.wait_ge(mlo_ok, 2 * t.img(o) + half + 1)
                for part in range(2):
                    sp.dma_start(qs[t.ring(o, 2)][KS + part:KS + part + 1, half * HC:(half + 1) * HC],
                                 mT[:, half, part]).then_inc(mrow_in[t.ring(o, 2)], 16)

            def stack_half(t, o, f):
                b = t.ring(o, 2)
                waits = [(parts_out, 32 * (t.img(o) + 1))]
                if t.before(o, 2):
                    waits += [(sc_ps, H * t.img(o - 2) + HALF * (f + 1))]
                wait_all(sp, *waits)
                heads = slice(f * HALF, (f + 1) * HALF)
                for stack, side, split in ((qs[b], 0, ((0, 3), (0, 2), (0, 1))), (ks[b], 1, ((0,) * 3, (1,) * 2, (2,)))):
                    row = 0
                    for run in split:
                        n = run[1] if side == 0 else len(run)
                        if side == 0:
                            src = parts_dram[b, side, 0:n, f]
                        else:
                            src = parts_dram[b, side, run[0]:run[0] + 1, f].to_broadcast([n, P, T])
                        sp.dma_start(stack[row:row + n * D, heads].rearrange("p h t -> p (h t)"),
                                     src.rearrange("a (d h) t -> a d (h t)", d=D)).then_inc(stack_in[b][f], 16)
                        row += n * D

            def slot(t):
                if t.has(1):
                    stack_half(t, 1, 1)
                if t.has(0):
                    max_rows(t, 0, 1)
                if t.has(2):
                    b = t.ring(2, 2)
                    waits = [(parts_ok, t.img(2) + 1)]
                    if t.before(2, 2):
                        waits += [(stack_in[b][1], STACK * (t.pair(0) + 1))]
                    wait_all(sp, *waits)
                    for side in range(2):
                        sp.dma_start(parts_dram[b, side].rearrange("a f p t -> p (a f) t"),
                                     parts[:, side].rearrange("p a f t -> p (a f) t")).then_inc(parts_out, 16)
                if t.has(1):
                    max_rows(t, 1, 0)
                if t.has(2):
                    stack_half(t, 2, 0)
                if t.has(-1):
                    sp.wait_ge(h2_ok, t.img(0))
                    sp.dma_start(h2_dram[t.img(-1)], h2[:, t.ring(-1, 2)].rearrange("p c e -> p (c e)")
                                 ).then_inc(h2_out, 16)
                if t.k == 0 and t.has_group(1):
                    waits = [(rec_ok, t.g + 2)]
                    if t.group_before(1, 1):
                        waits += [(xn_ok, t.img(GI)), (bo_ok, t.img(GI))]
                    wait_all(sp, *waits)
                    for i in range(GI):
                        for r in range(RP // QC):
                            sp.dma_start(h1[r::RP // QC, i].rearrange("p c e -> p (c e)"),
                                         img[i * IP:(i + 1) * IP, r * QC * E:(r + 1) * QC * E]
                                         ).then_inc(h1_in, 16)
                    if t.has_group(2):
                        sp.wait_ge(h1_in, H1_IN * (t.g + 2))
                        sp.dma_start(img[:], x_v[t.g + 2]).then_inc(x_in, 16)

            run(sp, slot)

            sp.wait_ge(h2_out, 16 * NI)
            sp.wait_ge(z_ok, NI)
            sp.wait_ge(pv_ps, 4 * NI)

            def slot2(t):
                if t.has(4):
                    if t.before(4, 8):
                        sp.wait_ge(c_y, t.img(-3))
                    sp.dma_start(hh[t.ring(4, 8)], h2_dram[t.img(4)]).then_inc(c_in[t.ring(4, 8)], 16)
                if t.has(-1):
                    sp.wait_ge(c_y, t.img(0))
                    sp.dma_start(out_v[t.img(-1)], oy[t.ring(-1, 4)]).then_inc(c_out[t.ring(-1, 4)], 16)
            run2(sp, slot2)
            for b in range(4):
                sp.wait_ge(c_out[b], 16 * (NI // 4))

        @block.gpsimd
        def _(pool):
            seq = Seq(pool, pool_seq, POOL_STEPS)
            pool.memset(ident[:], 0.0).then_inc(begun, 1)
            pool.memset(minus_half[:], -0.5).then_inc(made, 1)
            pool.wait_ge(begun, 1)
            pool.affine_select(out=ident[:], in_=ident[:], compare_op=ALU.not_equal, fill=1.0,
                               base=0, pattern=[[-1, P]], channel_multiplier=1).then_inc(made, 1)

            def views(l):
                r, c = BAND[l]
                half = sd[:, :, 0:2 * r * c]
                rows = half.rearrange("p s (r two c) -> p s r two c", two=2, c=c)
                cur = (img[:] if l == 0 else coef[l - 1][:, 0].rearrange("p r c -> p (r c)"))
                return cur.rearrange("p (n two) -> p n two", two=2), half, rows[:, :, :, 0], rows[:, :, :, 1]

            def forward(l, stage=None):
                cur, half, even, odd = views(l)
                if stage != 1:
                    pool.tensor_tensor(half[:, 0], cur[:, :, 0], cur[:, :, 1], ALU.add)
                    seq.link(pool.tensor_tensor(half[:, 1], cur[:, :, 0], cur[:, :, 1], ALU.subtract))
                if stage == 0:
                    return
                pool.tensor_tensor(coef[l][:, 0::2], even, odd, ALU.add)
                last = pool.tensor_tensor(coef[l][:, 1::2], even, odd, ALU.subtract)
                if l == 1:
                    seq.link_alone(last)
                else:
                    last.then_inc(fwd_done, 1)

            def inverse(l):
                cur, half, even, odd = views(l)
                pool.tensor_tensor(even, coef[l][:, 0::2], coef[l][:, 1::2], ALU.add)
                seq.link(pool.tensor_tensor(odd, coef[l][:, 0::2], coef[l][:, 1::2], ALU.subtract))
                pool.tensor_tensor(cur[:, :, 0], half[:, 0], half[:, 1], ALU.add)
                last = pool.tensor_tensor(cur[:, :, 1], half[:, 0], half[:, 1], ALU.subtract)
                if l:
                    seq.link(last)
                else:
                    last.then_inc(rec_ok, 1)

            def slot(t):
                if t.has(3):
                    wait_alone(pool, (var1_ok, t.img(3) + 1))
                    seq.link(pool.tensor_scalar(ve1[:], mv1[:, :, 1], LN_EPS, None, ALU.add))
                    pool.tensor_tensor(rstd1[:], ve1[:], minus_half[:], ALU.pow).then_inc(rstd1_ok, 1)
                if t.has(-2):
                    waits = [(var2_ok, t.img(-1))]
                    if t.before(-2, 1):
                        waits += [(z_ok, t.img(-2))]
                    wait_alone(pool, *waits)
                    var = mv2[:, :, 1]
                    seq.link(pool.tensor_scalar(rs2[:, 0], var, LN_EPS, None, ALU.add))
                    seq.link(pool.tensor_tensor(rs2[:, 1], rs2[:, 0], minus_half[:], ALU.pow))
                    seq.link(pool.tensor_tensor(rs2[:, 2], rs2[:, 1], rs2[:, 1], ALU.mult))
                    seq.link_alone(pool.tensor_tensor(rs2[:, 2], rs2[:, 2], var, ALU.mult))
                    seq.link(pool.tensor_scalar(rs2[:, 2], rs2[:, 2], FFN_LN_EPS, None, ALU.add))
                    seq.link(pool.tensor_tensor(rs2[:, 3], rs2[:, 2], minus_half[:], ALU.pow))
                    seq.link(pool.tensor_tensor(rs2[:, 4], rs2[:, 1], rs2[:, 3], ALU.mult))
                    seq.link_alone(pool.tensor_tensor(rs2[:, 2], rs2[:, 4], mv2[:, :, 0], ALU.mult))
                    pool.tensor_scalar(rs2[:, 2], rs2[:, 2], -1.0, None, ALU.mult).then_inc(rs2_ok, 1)
                if t.k == 3 and t.has_group(2):
                    pool.wait_ge(scaled, t.g + 3)
                    inverse(2)
                    inverse(1)
                if t.k == 1 and t.has_group(2):
                    pool.wait_ge(x_in, 16 * (t.g + 3))
                    forward(0, 0)
                if t.k == 2 and t.has_group(2):
                    pool.wait_ge(fwd_done, 2 * (t.g + 3) - 1)
                    forward(1)
                    forward(2)
                if t.has(2):
                    pool.wait_ge(mid_ok, t.img(2) + 1)
                    if t.before(2, 1):
                        pool.wait_ge(parts_out, 32 * t.img(2))
                    pool.tensor_tensor(parts[:, :, 2], qkr[:], parts[:, :, 1], ALU.subtract).then_inc(parts_ok, 1)
                if t.has(-2):
                    pool.wait_ge(z_ok, t.img(-1))
                    seq.link(pool.tensor_tensor(z[:], z[:], lng[:], ALU.mult))
                    pool.tensor_tensor(z[:], z[:], lnb[:], ALU.add).then_inc(zb_ok, 1)
                if t.k == 3 and t.has_group(2):
                    inverse(0)
                if t.k == 1 and t.has_group(2):
                    forward(0, 1)
                if t.has(3):
                    if t.before(3, GI):
                        pool.wait_ge(h2_ok, t.img(0))
                    pool.tensor_tensor(h1b[:, t.ring(3, GI)], h1[:, t.ring(3, GI)], bo_r[:], ALU.add).then_inc(bo_ok, 1)

            pool.wait_ge(consts_in, 16 * NCONST)
            run(pool, slot, seq)

            def slot2(t):
                if t.has(2):
                    pool.wait_ge(c_zg, t.img(2) + 1)
                    pool.tensor_tensor(zz[t.ring(2, GI)], zz[t.ring(2, GI)], lnb_v, ALU.add).then_inc(c_zb, 1)
            run2(pool, slot2)

        @block.scalar
        def _(act):
            def copy(out, in_, scale=1.0):
                return act.activation(out, in_, ACT.Copy, scale=scale)

            def max_high(t, o, half):
                act.wait_ge(mT_ps, 2 * t.img(o) + half + 1)
                if t.before(o, 1):
                    act.wait_ge(mrow_in[t.ring(o - 1, 2)], MROW * (t.pair(o - 1) + 1))
                copy(m32[:, half], ps_b[0:HC, 0:T])
                copy(mT[:, half, 0], ps_b[0:HC, 0:T]).then_inc(mhi_ok, 1)

            def evac_qk(t, side, ps, ready, done, scale):
                act.wait_ge(ready, t.img(2) + 1)
                if t.before(2, 1):
                    act.wait_ge(res_ok, t.img(2))
                    act.wait_ge(v_ps, t.img(2))
                    act.wait_ge(parts_out, 32 * t.img(2))
                copy(qk[:, side].rearrange("p c t -> p (c t)"), ps[:], scale)
                copy(parts[:, side, 0].rearrange("p c t -> p (c t)"), ps[:], scale).then_inc(done, 1)

            def evac_oT(t, o, bank):
                act.wait_ge(pv_ps, 4 * t.img(o) + 2 * bank + 2)
                if t.before(o, 1):
                    act.wait_ge(o1_ps, 2 * t.img(o - 1) + bank + 1)
                copy(oT[:, 2 * bank:2 * bank + 2].rearrange("p q t -> p (q t)"), ps_o[bank][:]).then_inc(oT_ok, 1)

            def slot(t):
                for h in range(H):
                    if t.has(0):
                        act.wait_ge(sc_ps, H * t.img(0) + h + 1)
                        if h >= 8 or t.before(0, 1):
                            act.wait_ge(pv_ps, 4 * t.img(0) + h // 4 - 1)
                        act.activation(prob[:, h % 8].rearrange("p c t -> p (c t)"), ps_s[h % 2][:],
                                       ACT.Exp).then_inc(exp_ok, 1)
                    if h == 0 and t.has(2):
                        act.wait_ge(xnT_ps, t.img(2) + 1)
                        if t.before(2, 1):
                            act.wait_ge(qT_ps, t.img(2))
                        copy(xnT[:].rearrange("p c t -> p (c t)"), ps_a[:]).then_inc(xnT_ok, 1)
                    if h == 1 and t.has(0):
                        max_high(t, 0, 1)
                    if h == 2 and t.has(2):
                        evac_qk(t, 1, ps_a, kT_ps, kT_ok, 1.0)
                    if h == 3 and t.has(2):
                        evac_qk(t, 0, ps_b, qT_ps, qT_ok, SCALE)
                    if h == 4 and t.has(-1):
                        evac_oT(t, -1, 1)
                    if h == 5 and t.has(2):
                        act.wait_ge(v_ps, t.img(2) + 1)
                        if t.before(2, GI):
                            act.wait_ge(pv_ps, 4 * t.img(-1))
                        for c in range(QC):
                            last = copy(vaug[:, t.ring(2, GI), c, :, 0:D].rearrange("p (f h) d -> p f h d", f=EC),
                                        ps_a[:, c * E:(c + 1) * E].rearrange("p (f d h) -> p f h d", f=EC, d=D))
                        last.then_inc(v_ok, 1)
                    if h == 6 and t.has(2):
                        act.wait_ge(res_ok, t.img(2) + 1)
                        copy(parts[:, :, 1], qkr[:]).then_inc(mid_ok, 1)
                    if h == 9 and t.has(1):
                        max_high(t, 1, 0)
                    if h == 10 and t.has(0):
                        evac_oT(t, 0, 0)
                    if h == 11 and t.has(-1):
                        act.wait_ge(attT_ps, t.img(0))
                        if t.before(-1, 1):
                            act.wait_ge(proj_ps, t.img(-1))
                        copy(attT[:].rearrange("p c t -> p (c t)"), ps_a[:]).then_inc(attT_ok, 1)
                    if h == 14 and t.k == 2 and t.has_group(2):
                        act.wait_ge(glog_ok, t.g + 3)
                        act.activation(gexp[:], glog[:], ACT.Exp).then_inc(gexp_ok, 1)
                    if h == 0 and t.k == 3 and t.has_group(2):
                        act.wait_ge(gate_ok, t.g + 3)
                        for l in range(LEVELS):
                            for band in range(3):
                                copy(coef[l][:, 1 + band], coef[l][:, 1 + band], gate[:, 3 * l + band:3 * l + band + 1])
                        copy(coef[2][:, 0], coef[2][:, 0], gate[:, 9:10]).then_inc(scaled, 1)

            run(act, slot)

            def slot2(t):
                if t.has(3):
                    i, b = t.img(3), t.ring(3, GI)
                    if t.before(3, GI):
                        act.wait_ge(c_t_ps, t.img(0))
                    act.wait_ge(c_in[t.ring(3, 8)], 16 * (t.turn(3, 8) + 1))
                    for c in range(QC):
                        e = slice(c * E, (c + 1) * E)
                        last = act.activation(zz[b][:, e], hh[t.ring(3, 8)][:, e], ACT.Identity,
                                              bias=stats[:, i, 0, c:c + 1], scale=stats[:, i, 1, c:c + 1])
                    last.then_inc(c_z, 1)
                if t.has(0):
                    act.wait_ge(c_t_ps, t.img(0) + 1)
                    if t.before(0, 2):
                        act.wait_ge(c_y_ps, t.img(-1))
                    copy(xT[t.ring(0, 2)], ps_s[t.ring(0, 2)][:]).then_inc(c_t, 1)
            run2(act, slot2)

        @block.vector
        def _(dve):
            seq = Seq(dve, dve_seq, DVE_STEPS)
            link = seq.link
            dve.memset(ones[:], 1.0).then_inc(made, 1)
            link(dve.memset(blk1[:], 0.0))
            for i in range(GI):
                dve.memset(blk1[i * IP:(i + 1) * IP, i * IP:(i + 1) * IP], 1.0).then_inc(made, 1)
            for b in range(2):
                dve.memset(ks[b][KS:P], 1.0).then_inc(made, 1)
            dve.memset(vaug[:], 1.0).then_inc(made, 1)
            link(dve.memset(zmax[:], 0.0))
            dve.wait_ge(consts_in, 16 * NCONST)

            def ternary():
                link(dve.tensor_reduce(fs[:, 0:1], wf[:].rearrange("p c n -> p (c n)"), AX.X, ALU.add,
                                       apply_absolute_value=True))
                dve.wait_ge(made, MADE)
                dve.nop().then_inc(prep_ok, 1)
                dve.wait_ge(prep_ps, 1)
                link(dve.tensor_scalar(fs[:, 1:2], ps_a[:, 0:1], 1.0 / (E * E), None, ALU.mult))
                link(dve.tensor_scalar(fs[:, 2:3], fs[:, 1:2], FFN_EPS, None, ALU.add))
                link(dve.reciprocal(fs[:, 3:4], fs[:, 2:3]))
                link(dve.tensor_scalar(wf[:], wf[:], fs[:, 3:4], 1.0, ALU.mult, ALU.min))
                link(dve.tensor_scalar(wf[:], wf[:], -1.0, ROUND, ALU.max, ALU.add))
                link(dve.tensor_scalar(wf[:], wf[:], -ROUND, None, ALU.add))

            def gate_product(n):
                if n < 3 * LEVELS:
                    l, o = divmod(n, 3)
                    r, c = BAND[l]
                    data = coef[l][:, 1:4].rearrange("p b r c -> p (b r c)")
                    w = gw[l][:].rearrange("p b f o -> p (b f) o")[:, :, o]
                else:
                    r, c = BAND[LEVELS - 1]
                    data, w = coef[LEVELS - 1][:, 0].rearrange("p r c -> p (r c)"), gwa[:]
                size = data.shape[1]
                junk = img[:, 0:size]
                return dve.tensor_tensor_reduce(out=junk, in0=data, in1=w, scale=1.0, scalar=0.0,
                                                op0=ALU.mult, op1=ALU.add, accum_out=gpart[:, n:n + 1])

            def gate_logits():
                for l in range(LEVELS):
                    q = slice(3 * l, 3 * l + 3 + (l == LEVELS - 1))
                    last = dve.scalar_tensor_tensor(glog[:, q], ps_a[:, q], 0.5 ** (l + 1), gbias[:, q],
                                                    ALU.mult, ALU.add)
                link(last)
                v = glog[:, 0:9].rearrange("p (l b) -> p l b", b=3)
                link(dve.tensor_reduce(gmx[:], v, AX.X, ALU.max))
                dve.tensor_tensor(v, v, gmx[:].unsqueeze(2).to_broadcast([P, 3, 3]), ALU.subtract)
                dve.tensor_scalar(glog[:, 9:10], glog[:, 9:10], -1.0, None, ALU.mult).then_inc(glog_ok, 1)

            def gate_values(g3):
                dve.wait_ge(gexp_ok, g3)
                v = gexp[:, 0:9].rearrange("p (l b) -> p l b", b=3)
                dve.tensor_reduce(gsum[:, 0:3], v, AX.X, ALU.add)
                link(dve.tensor_scalar(gsum[:, 3:4], gexp[:, 9:10], 1.0, None, ALU.add))
                link(dve.reciprocal(grec[:], gsum[:]))
                for l in range(LEVELS):
                    dve.tensor_scalar(gate[:, 3 * l:3 * l + 3], gexp[:, 3 * l:3 * l + 3], grec[:, l:l + 1],
                                      0.25 ** (l + 1), ALU.mult, ALU.mult)
                dve.tensor_scalar(gate[:, 9:10], grec[:, 3:4], 0.25 ** LEVELS, None, ALU.mult).then_inc(gate_ok, 1)

            def max_low(t, o, half):
                dve.wait_ge(mhi_ok, 2 * t.img(o) + half + 1)
                dve.tensor_tensor(mT[:, half, 1], m32[:, half], mT[:, half, 0], ALU.subtract).then_inc(mlo_ok, 1)

            def piece(t, o, n):
                pair, c = divmod(n, QC)
                half, j = divmod(pair, 4)
                dve.wait_ge(msc_ps, H * t.img(o) + n + 1)
                if n % 8 == 0 and t.before(o, 1):
                    dve.wait_ge(mT_ps, 2 * t.img(o - 1) + half + 1)
                dve.tensor_reduce(negm[:, half, c, 2 * j:2 * j + 2], ps_m[n % 2][:].rearrange("p (j t) -> p j t", j=2),
                                  AX.X, ALU.max, negate=True).then_inc(max_ok, 1)

            def normalise(t, bank, ps):
                v = ps[:].rearrange("p (qc j w) -> p qc j w", j=4, w=2 * D)
                dve.wait_ge(o1_ps, 2 * t.img(-1) + bank + 1)
                link(dve.reciprocal(rden[:, bank].rearrange("p q c j -> p (q c) j"), v[:, :, :, D]))
                if bank == 0 and t.before(-1, 1):
                    dve.wait_ge(attT_ps, t.img(-1))
                v5 = v.rearrange("p (q c) j w -> p q c j w", c=QC)
                for c in range(QC):
                    last = dve.tensor_tensor(
                        att[:, c, bank * P:(bank + 1) * P].rearrange("p (q j d) -> p q j d", q=2, j=4),
                        v5[:, :, c, :, 0:D], rden[:, bank, :, c].unsqueeze(3).to_broadcast([P, 2, 4, D]), ALU.mult)
                last.then_inc(att_ok, 1)

            def slot(t):
                for h in range(H):
                    if t.has(1):
                        piece(t, 1, h)
                    if h == 2 and t.has(0):
                        max_low(t, 0, 1)
                    if h == 3 and t.has(-2):
                        dve.wait_ge(rs2_ok, t.img(-1))
                        for c in range(QC):
                            last = dve.tensor_scalar(z[:, c], h2[:, t.ring(-2, 2), c], mv2[:, c, 0:1],
                                                     rs2[:, 4, c:c + 1], ALU.subtract, ALU.mult)
                        dve.tensor_copy(stats[:, t.img(-2), 0], rs2[:, 2])
                        dve.tensor_copy(stats[:, t.img(-2), 1], rs2[:, 4]).then_inc(z_ok, 1)
                    if h == 12 and t.has(-2):
                        dve.wait_ge(zb_ok, t.img(-1))
                        link(dve.tensor_reduce(zmax[:, 1:2], z[:].rearrange("p c e -> p (c e)"), AX.X, ALU.max,
                                               apply_absolute_value=True))
                        link(dve.tensor_tensor(zmax[:, 0:1], zmax[:, 0:1], zmax[:, 1:2], ALU.max))
                    if h == 4 and t.has(2):
                        dve.wait_ge(kT_ok, t.img(2) + 1)
                        dve.wait_ge(qT_ok, t.img(2) + 1)
                        if t.before(2, 1):
                            dve.wait_ge(parts_ok, t.img(2))
                        dve.tensor_tensor(qkr[:], qk[:], parts[:, :, 0], ALU.subtract).then_inc(res_ok, 1)
                    if t.k == 2 and h < 10 and t.has_group(2):
                        if h == 0:
                            dve.wait_ge(fwd_done, 2 * (t.g + 3) - 1)
                        if h == 3:
                            dve.wait_ge(fwd_done, 2 * (t.g + 3))
                        if h == 9:
                            gate_product(h).then_inc(gprod, 1)
                        else:
                            link(gate_product(h))
                    if h == 7 and t.has(-1):
                        normalise(t, 0, ps_b)
                    if h == 8 and t.has(-1):
                        normalise(t, 1, ps_a)
                    if h == 10 and t.has(1):
                        max_low(t, 1, 0)
                    if h == 0 and t.has(3):
                        if t.ring(3, GI) == 0:
                            dve.wait_ge(h1_in, H1_IN * ((t.g + (t.k + 3) // GI) + 1))
                        for c in range(QC):
                            last = dve.bn_stats(bn[:, c], h1[:, t.ring(3, GI), c])
                        if t.before(3, 1):
                            dve.wait_ge(rstd1_ok, t.img(3))
                        seq.link_alone(last)
                        for c in range(QC):
                            last = dve.bn_aggr(mv1[:, c], bn[:, c])
                        last.then_inc(var1_ok, 1)
                    if h == 6 and t.has(3):
                        dve.wait_ge(rstd1_ok, t.img(3) + 1)
                        if t.before(3, 2):
                            dve.wait_ge(xnT_ps, t.img(2))
                        for c in range(QC):
                            last = dve.tensor_scalar(xn[:, t.ring(3, 2), c], h1[:, t.ring(3, GI), c],
                                                     mv1[:, c, 0:1], rstd1[:, c:c + 1], ALU.subtract, ALU.mult)
                        last.then_inc(xn_ok, 1)
                    if h == 13 and t.has(-1):
                        b = t.ring(-1, 2)
                        dve.wait_ge(proj_ps, t.img(0))
                        dve.wait_ge(bo_ok, t.img(0))
                        if t.before(-1, 2):
                            dve.wait_ge(h2_out, 16 * t.img(-1))
                        dve.tensor_tensor(h2[:, b].rearrange("p c e -> p (c e)"), ps_b[:],
                                          h1b[:, t.ring(-1, GI)].rearrange("p c e -> p (c e)"), ALU.add).then_inc(h2_ok, 1)
                        dve.wait_ge(h2_ok, t.img(0))
                        for c in range(QC):
                            last = dve.bn_stats(bn[:, c], h2[:, b, c])
                        if t.before(-1, 1):
                            dve.wait_ge(rs2_ok, t.img(-1))
                        seq.link_alone(last)
                        for c in range(QC):
                            last = dve.bn_aggr(mv2[:, c], bn[:, c])
                        last.then_inc(var2_ok, 1)
                    if h == 13 and t.k == 2 and t.has_group(2):
                        dve.wait_ge(glog_ps, t.g + 3)
                        gate_logits()
                    if h == 14 and t.k == 2 and t.has_group(2):
                        gate_values(t.g + 3)

            for side, w in enumerate((wq, wk)):
                dve.tensor_copy(w[:].rearrange("p e (f d h) -> p (e f) d h", f=EC, d=D),
                                h2[:, side].rearrange("p e (f h d) -> p (e f) d h", f=EC, d=D)).then_inc(made, 1)
            ternary()
            run(dve, slot, seq)

            dve.nop().then_inc(prep_ok, 1)
            dve.wait_ge(prep_ps, 2)
            link(dve.tensor_reduce(zrow[:, 0:1], ps_a[0:1, 0:P], AX.X, ALU.max))
            dve.nop().then_inc(prep_ok, 1)
            dve.wait_ge(prep_ps, 3)
            link(dve.tensor_scalar(fs[:, 4:5], ps_b[:, 0:1], 1.0, None, ALU.mult))
            link(dve.reciprocal(fs[:, 5:6], fs[:, 4:5]))
            link(dve.tensor_scalar(fs[:, 5:6], fs[:, 5:6], QB, None, ALU.mult))
            link(dve.tensor_scalar(fs[:, 6:7], fs[:, 4:5], fs[:, 1:2], 1.0 / QB, ALU.mult, ALU.mult))

            def slot2(t):
                if t.has(2):
                    b = t.ring(2, GI)
                    dve.wait_ge(c_z, t.img(2) + 1)
                    dve.tensor_tensor(zz[b], zz[b], lng_v, ALU.mult).then_inc(c_zg, 1)
                if t.has(1):
                    b = t.ring(1, GI)
                    dve.wait_ge(c_zb, t.img(1) + 1)
                    dve.tensor_scalar(zz[b], zz[b], fs[:, 5:6], CLIP, ALU.mult, ALU.min).then_inc(c_cl, 1)
                if t.has(-1):
                    b = t.ring(-1, 2)
                    dve.wait_ge(c_y_ps, t.img(0))
                    if t.before(-1, GI):
                        dve.wait_ge(c_out[t.ring(-1, 4)], 16 * t.turn(-1, 4))
                    dve.scalar_tensor_tensor(oy[t.ring(-1, 4)], ps_m[b][:], fs[:, 6:7], hh[t.ring(-1, 8)],
                                             ALU.mult, ALU.add).then_inc(c_y, 1)
                if t.has(1):
                    b = t.ring(1, GI)
                    dve.wait_ge(c_cl, t.img(1) + 1)
                    dve.tensor_scalar(zz[b], zz[b], -CLIP, None, ALU.max).then_inc(c_x, 1)
            run2(dve, slot2)

        @block.tensor
        def _(pe):
            def transposes(t, ps, tile):
                for e in range(2):
                    for c in range(2):
                        last = pe.transpose(ps[:, e * T + c * P:e * T + (c + 1) * P], tile[:, c, e * P:(e + 1) * P],
                                            ident[:])
                return last

            def project(ps, w):
                for f in range(EC):
                    for e in range(EC):
                        last = pe.matmul(ps[:, f * T:(f + 1) * T],
                                         w[:, e, f * P:(f + 1) * P], xnT[:, e], start=(e == 0), stop=(e == EC - 1))
                return last

            def maxima_rows(t, o, half):
                pe.wait_ge(max_ok, H * t.img(o) + 8 * (half + 1))
                for c in range(QC):
                    last = pe.transpose(ps_b[0:HC, c * P:(c + 1) * P], negm[:, half, c], ident[:])
                last.then_inc(mT_ps, 1)

            def piece(t, o, n):
                pair, c = divmod(n, QC)
                if n % HALF == 0:
                    pe.wait_ge(stack_in[t.ring(o, 2)][n // HALF], STACK * (t.pair(o) + 1))
                if n >= 2 or t.before(o, 1):
                    pe.wait_ge(max_ok, H * t.img(o) + n - 1)
                for j in range(2):
                    q = qs[t.ring(o, 2)][0:KS, 2 * pair + j, c * P:(c + 1) * P]
                    last = pe.matmul(ps_m[n % 2][:, j * T:(j + 1) * T], q, ks[t.ring(o, 2)][0:KS, 2 * pair + j],
                                     start=True, stop=True)
                last.then_inc(msc_ps, 1)

            def values(t, o, quad):
                if quad == 0:
                    pe.wait_ge(v_ok, t.img(o) + 1)
                pe.wait_ge(exp_ok, H * t.img(o) + 4 * (quad + 1))
                if quad % 2 == 0 and t.before(o, 1):
                    pe.wait_ge(oT_ok, 2 * t.img(o - 1) + quad // 2 + 1)
                for c in range(QC):
                    for j in range(4):
                        last = pe.matmul(ps_o[quad // 2][j * 2 * D:(j + 1) * 2 * D, (quad % 2) * T:(quad % 2 + 1) * T],
                                         vaug[:, t.ring(o, GI), c, 4 * quad + j], prob[:, (4 * quad + j) % 8, c],
                                         start=(c == 0), stop=(c == QC - 1))
                last.then_inc(pv_ps, 1)

            def tokens(t, bank, ps):
                pe.wait_ge(oT_ok, 2 * t.img(-1) + bank + 1)
                for q in range(2):
                    for c in range(QC):
                        last = pe.transpose(ps[:, (q * QC + c) * P:(q * QC + c + 1) * P],
                                            oT[:, 2 * bank + q, c * P:(c + 1) * P], ident[:])
                last.then_inc(o1_ps, 1)

            def slot(t):
                for h in range(H):
                    if t.has(0):
                        if h % HC == 0:
                            pe.wait_ge(mrow_in[t.ring(0, 2)], MROW * t.pair(0) + 32 * (h // HC + 1))
                        if h >= 2 or t.before(0, 1):
                            pe.wait_ge(exp_ok, H * t.img(0) + h - 1)
                        for c in range(QC):
                            last = pe.matmul(ps_s[h % 2][:, c * T:(c + 1) * T],
                                             ks[t.ring(0, 2)][0:KM, h, c * P:(c + 1) * P], qs[t.ring(0, 2)][0:KM, h],
                                             start=True, stop=True)
                        last.then_inc(sc_ps, 1)
                    if t.has(1):
                        piece(t, 1, h)
                    if h == 1 and t.has(-1):
                        values(t, -1, 3)
                    if h in (5, 9, 13) and t.has(0):
                        values(t, 0, (h - 5) // 4)
                    if h == 0 and t.has(2):
                        if t.has(-2):
                            pe.wait_ge(attT_ok, t.img(-1))
                        elif t.has(1):
                            pe.wait_ge(v_ok, t.img(2))
                        if t.k == 3 and t.has_group(2):
                            pe.wait_ge(glog_ok, t.g + 3)
                        pe.wait_ge(xn_ok, t.img(2) + 1)
                        transposes(t, ps_a, xn[:, t.ring(2, 2)]).then_inc(xnT_ps, 1)
                    if h == 1 and t.has(0):
                        if t.has(-2):
                            pe.wait_ge(h2_ok, t.img(-1))
                        else:
                            pe.wait_ge(mhi_ok, 2 * t.img(0) + 1)
                        maxima_rows(t, 0, 1)
                    if h == 2 and t.has(2):
                        pe.wait_ge(xnT_ok, t.img(2) + 1)
                        project(ps_a, wk).then_inc(kT_ps, 1)
                    if h == 3 and t.has(2):
                        if t.has(0):
                            pe.wait_ge(mhi_ok, 2 * t.img(0) + 2)
                        elif t.has(1):
                            pe.wait_ge(qT_ok, t.img(2))
                        project(ps_b, wq).then_inc(qT_ps, 1)
                    if h == 5 and t.has(2):
                        pe.wait_ge(kT_ok, t.img(2) + 1)
                        transposes_kT(t)
                    if h == 6 and t.has(-1):
                        if t.has(2):
                            pe.wait_ge(qT_ok, t.img(2) + 1)
                        elif t.has(0):
                            pe.wait_ge(mhi_ok, 2 * t.img(0) + 2)
                        else:
                            pe.wait_ge(h2_ok, t.img(-1))
                        tokens(t, 0, ps_b)
                    if h == 7 and t.has(-1):
                        if t.has(2):
                            pe.wait_ge(v_ok, t.img(2) + 1)
                        else:
                            pe.wait_ge(attT_ok, t.img(-1))
                        tokens(t, 1, ps_a)
                    if h == 9 and t.has(1):
                        if t.has(-1):
                            pe.wait_ge(att_ok, 2 * t.img(-1) + 1)
                        else:
                            pe.wait_ge(qT_ok, t.img(2) + 1)
                        maxima_rows(t, 1, 0)
                    if h == 10 and t.has(-1):
                        pe.wait_ge(att_ok, 2 * t.img(0))
                        transposes(t, ps_a, att).then_inc(attT_ps, 1)
                    if h == 12 and t.has(-1):
                        pe.wait_ge(attT_ok, t.img(0))
                        if t.has(1):
                            pe.wait_ge(mhi_ok, 2 * t.img(1) + 1)
                        for c in range(QC):
                            for e in range(EC):
                                last = pe.matmul(ps_b[:, c * E:(c + 1) * E], attT[:, e, c * P:(c + 1) * P], wo[:, e],
                                                 start=(e == 0), stop=(e == EC - 1))
                        last.then_inc(proj_ps, 1)
                    if h == 12 and t.k == 2 and t.has_group(2):
                        pe.wait_ge(gprod, t.g + 3)
                        if t.has(-1):
                            pe.wait_ge(attT_ok, t.img(0))
                        elif t.has(2):
                            pe.wait_ge(v_ok, t.img(2) + 1)
                        pe.matmul(ps_a[:, 0:10], blk1[:], gpart[:], start=True, stop=True).then_inc(glog_ps, 1)

            def transposes_kT(t):
                for c in range(QC):
                    for f in range(EC):
                        last = pe.transpose(ps_a[:, (c * EC + f) * P:(c * EC + f + 1) * P],
                                            qk[:, 1, f, c * P:(c + 1) * P], ident[:])
                last.then_inc(v_ps, 1)

            pe.wait_ge(made, MADE)
            pe.wait_ge(consts_in, 16 * NCONST)
            pe.wait_ge(prep_ok, 1)
            pe.matmul(ps_a[:, 0:1], ones[:], fs[:, 0:1], start=True, stop=True).then_inc(prep_ps, 1)
            pe.wait_ge(dve_seq, 4)
            run(pe, slot)
            pe.wait_ge(prep_ok, 2)
            pe.transpose(ps_a[0:1, 0:P], zmax[:, 0:1], ident[:]).then_inc(prep_ps, 1)
            pe.wait_ge(prep_ok, 3)
            pe.matmul(ps_b[:, 0:1], ones[0:1, :], zrow[:, 0:1], start=True, stop=True).then_inc(prep_ps, 1)

            def slot2(t):
                if t.has(1):
                    b = t.ring(1, 2)
                    pe.wait_ge(c_x, t.img(1) + 1)
                    if t.before(1, 2):
                        pe.wait_ge(c_t, t.img(0))
                    x_ = zz[t.ring(1, GI)].rearrange("p (c e) -> p c e", c=QC)
                    transposes(t, ps_s[b], x_).then_inc(c_t_ps, 1)
                if t.has(0):
                    b = t.ring(0, 2)
                    pe.wait_ge(c_t, t.img(0) + 1)
                    if t.before(0, 2):
                        pe.wait_ge(c_y, t.img(-1))
                    for c in range(QC):
                        for e in range(EC):
                            last = pe.matmul(ps_m[b][:, c * E:(c + 1) * E],
                                             xT[b][:, e * T + c * P:e * T + (c + 1) * P],
                                             wf[:, e], start=(e == 0), stop=(e == EC - 1))
                    last.then_inc(c_y_ps, 1)
            run2(pe, slot2)


_INS = ["x", "L0_tok_Wa", "L0_tok_ba", "L0_tok_Wd1", "L0_tok_bd1", "L0_tok_Wd2", "L0_tok_bd2", "L0_tok_Wd3",
        "L0_tok_bd3", "L0_attn_Wk", "L0_attn_Wq", "L0_attn_Wo", "L0_attn_bo", "L0_ffn_weight", "L0_ffn_ln_gamma",
        "L0_ffn_ln_beta"]


def kernel(**inputs):
    import numpy as np
    import concourse.bacc as bacc
    from concourse.bass_utils import run_bass_kernel_spmd

    nc = bacc.Bacc("TRN2", target_bir_lowering=False, num_devices=1)
    arrays, args = {}, []
    for name in _INS:
        a = np.ascontiguousarray(inputs[name])
        arrays[name] = a
        args.append(nc.dram_tensor(name, a.shape, mybir.dt.from_np(a.dtype), kind="ExternalInput").ap())
    out = nc.dram_tensor("out", (NI, T, E), F32, kind="ExternalOutput").ap()
    build(nc, *args, out)
    return run_bass_kernel_spmd(nc, [arrays], core_ids=[0]).results[0]["out"]
```

```python
import concourse.bass as bass
from concourse import mybir
from contextlib import ExitStack

F32 = mybir.dt.float32
BF16 = mybir.dt.bfloat16
ALU = mybir.AluOpType
ACT = mybir.ActivationFunctionType
AX = mybir.AxisListType

P = 128
NI = 32
T = 256
E = 256
H = 16
D = E // H
GI = 4
NG = NI // GI
IP = P // GI
RP = T // IP
EC = E // P
QC = T // P
HC = H // EC
PARTS = 3
Q_PARTS = (0, 1, 0, 1, 0, 2)
K_PARTS = (2, 1, 1, 0, 0, 0)
assert sorted(zip(Q_PARTS, K_PARTS)) == [(q, k) for q in range(PARTS) for k in range(PARTS - q)]
KS = len(Q_PARTS) * D
KM = KS + 2
SCALE = (E ** -0.25) ** 2
LN_EPS = 1e-5
FFN_LN_EPS = 1e-3
FFN_EPS = 1e-5
QB = 128.0
CLIP = QB - FFN_EPS
ROUND = 1.5 * 2.0 ** 23
LEVELS = 3
BAND = [(RP >> (l + 1), E >> (l + 1)) for l in range(LEVELS)]

STACK = 16 * 4
MROW = 16 * 2 * 2
H1_IN = 16
MADE = 2 + (GI + 3)
POOL_STEPS = 49
DVE_STEPS = 32

PART = ((0, 1, 2), (2, 1, 0))
GATE_STEPS = {(1, 4): (0,), (1, 5): (1,), (1, 9): (2,), (1, 11): (3,), (1, 12): (4,), (1, 14): (5,),
              (2, 2): (6, 9), (2, 3): (7, 10), (2, 4): (8, 11), (2, 5): (12,)}
FIRST_GATE_STEPS = {(1, 10): (0, 1, 2), (2, 3): (3,), (2, 5): (4, 5), (2, 7): (6, 9, 7), (2, 8): (10, 8, 11, 12)}
SCALE_STEPS = {(2, 12): (2, (0, 1, 2)), (2, 13): (1, (0, 1, 2)), (2, 14): (0, (0,)), (2, 15): (0, (1,)),
               (3, 0): (0, (2,))}
HALF = H // 2


def build(nc, x, Wa, ba, Wd1, bd1, Wd2, bd2, Wd3, bd3, Wk, Wq, Wo, bo, Wf, ln_g, ln_b, out):
    parts_dram = nc.dram_tensor("parts_scratch", (2, 2, EC, PARTS, P, T), BF16, kind="Internal").ap()
    h2_dram = nc.dram_tensor("h2_scratch", (NI, P, QC * E), F32, kind="Internal").ap()
    x_v = x.rearrange("(g i) (p r) w c -> g (i p) (r w c)", i=GI, r=RP)
    out_v = out.rearrange("b (p c) e -> b p (c e)", c=QC)

    ctx = ExitStack()
    with ctx:
        def sb(name, shape, dt=F32):
            return ctx.enter_context(nc.sbuf_tensor(name, shape, dt))

        def pb(name, shape=(P, 512)):
            return ctx.enter_context(nc.psum_tensor(name, list(shape), F32))

        def sem(name):
            return ctx.enter_context(nc.semaphore(name))

        img = sb("img", [P, RP * E])
        rec = sb("rec", [P, RP * E])
        sd = sb("sd", [P, 2, RP * E // 2])
        coef = [sb(f"coef{l}", [P, 4, r, c]) for l, (r, c) in enumerate(BAND)]
        gw = [sb(f"gw{l}", [P, 3, r * c, 3]) for l, (r, c) in enumerate(BAND)]
        gwa = sb("gwa", [P, BAND[2][0] * BAND[2][1]])
        gbias = sb("gbias", [P, 10])
        gpart = sb("gpart", [P, 2, 10])
        glog = sb("glog", [P, 10])
        gmx = sb("gmx", [P, 3])
        gexp = sb("gexp", [P, 10])
        gsum = sb("gsum", [P, 4])
        grec = sb("grec", [P, 4])
        gate = sb("gate", [P, 10])
        h1 = sb("h1", [P, GI, QC, E])
        h1b = sb("h1b", [P, GI, QC, E])
        bn1 = sb("bn1", [P, QC, 6])
        bn2 = sb("bn2", [P, QC, 6])
        mv1 = sb("mv1", [P, QC, 2])
        ve1 = sb("ve1", [P, QC])
        rstd1 = sb("rstd1", [P, QC])
        xn = sb("xn", [P, 2, QC, E])
        xnT = sb("xnT", [P, EC, T])
        qk = sb("qk", [P, 2, EC, T])
        qkr = sb("qkr", [P, 2, EC, T])
        parts = sb("parts", [P, 2, EC, PARTS, T], BF16)
        qs = [sb(f"qs{b}", [P, H, T], BF16) for b in range(2)]
        ks = [sb(f"ks{b}", [P, H, T], BF16) for b in range(2)]
        vaug = sb("vaug", [P, GI, QC, H, 2 * D])
        negm = sb("negm", [P, 2, QC, H // 2])
        m32 = sb("m32", [H // 2, T])
        mT = sb("mT", [H // 2, 2, 2, T], BF16)
        prob = sb("prob", [P, 8, QC, T])
        oT = sb("oT", [P, 4, T])
        rden = sb("rden", [P, 2, 2, QC, 4])
        att = sb("att", [P, QC, E])
        attT = sb("attT", [P, EC, T])
        h2 = sb("h2", [P, 2, QC, E])
        mv2 = sb("mv2", [P, QC, 2])
        rs2 = sb("rs2", [P, 5, QC])
        stats = sb("stats", [P, NI, 2, QC])
        z = sb("z", [P, QC, E])
        zmax = sb("zmax", [P, 3])
        wq = sb("wq", [P, EC, E])
        wk = sb("wk", [P, EC, E])
        wo = sb("wo", [P, EC, E])
        wf = sb("wf", [P, EC, E])
        ident = sb("ident", [P, P])
        ones = sb("ones", [P, P])
        blk1 = sb("blk1", [P, P])
        bo_r = sb("bo_r", [P, E])
        lng = sb("lng", [P, E])
        lnb = sb("lnb", [P, E])
        minus_half = sb("minus_half", [P, QC])
        fs = sb("fs", [P, 8])
        zrow = sb("zrow", [1, P])

        hh = [prob[:, b].rearrange("p c e -> p (c e)") for b in range(8)]
        zz = [vaug[:, b].rearrange("p c h d -> p (c h d)")[:, 0:QC * E] for b in range(GI)]
        xT = [attT[:].rearrange("p c t -> p (c t)"), xnT[:].rearrange("p c t -> p (c t)")]
        oy = [h1[:, b].rearrange("p c e -> p (c e)") for b in range(GI)]

        bo_v, lng_v, lnb_v = (r[:].unsqueeze(1).to_broadcast([P, QC, E]) for r in (bo_r, lng, lnb))

        ps_s = [pb(f"ps_s{b}") for b in range(2)]
        ps_m = [pb(f"ps_m{b}") for b in range(3)]
        ps_o = pb("ps_o")
        ps_a, ps_b = pb("ps_a"), pb("ps_b")

        consts_in = sem("consts_in")
        gates_in = sem("gates_in")
        w_ok = sem("w_ok")
        mean_ok = sem("mean_ok")
        x_in = sem("x_in")
        h1_in = [sem(f"h1_in{i}") for i in range(GI)]
        begun = sem("begun")
        made = sem("made")
        dve_seq = sem("dve_seq")
        pool_seq = sem("pool_seq")
        fwd_done = sem("fwd_done")
        gprod = sem("gprod")
        glog_ps = sem("glog_ps")
        glog_ok = sem("glog_ok")
        gexp_ok = sem("gexp_ok")
        gate_ok = sem("gate_ok")
        scaled = sem("scaled")
        rec_ok = sem("rec_ok")
        var1_ok = sem("var1_ok")
        rstd1_ok = sem("rstd1_ok")
        xn_ok = sem("xn_ok")
        bo_ok = sem("bo_ok")
        xnT_ps = sem("xnT_ps")
        xnT_ok = sem("xnT_ok")
        kT_ps = sem("kT_ps")
        kT_ok = sem("kT_ok")
        qT_ps = sem("qT_ps")
        qT_ok = sem("qT_ok")
        res_ok = sem("res_ok")
        mid_ok = sem("mid_ok")
        parts_ok = sem("parts_ok")
        parts_out = sem("parts_out")
        stack_in = [[sem(f"stack_in{b}{f}") for f in range(2)] for b in range(2)]
        v_ps = sem("v_ps")
        v_ok = sem("v_ok")
        msc_ps = sem("msc_ps")
        max_ok = sem("max_ok")
        mT_ps = sem("mT_ps")
        mhi_ok = sem("mhi_ok")
        mlo_ok = sem("mlo_ok")
        mrow_in = [sem(f"mrow_in{b}") for b in range(2)]
        sc_ps = sem("sc_ps")
        exp_ok = sem("exp_ok")
        pv_ps = sem("pv_ps")
        oT_ok = sem("oT_ok")
        o1_ps = sem("o1_ps")
        att_ok = sem("att_ok")
        attT_ps = sem("attT_ps")
        attT_ok = sem("attT_ok")
        proj_ps = sem("proj_ps")
        h2_ok = sem("h2_ok")
        var2_ok = sem("var2_ok")
        rs2_ok = sem("rs2_ok")
        z_ok = sem("z_ok")
        zb_ok = sem("zb_ok")
        zmax_ok = sem("zmax_ok")
        stat_ok = sem("stat_ok")
        h2_out = sem("h2_out")
        prep_ps = sem("prep_ps")
        prep_ok = sem("prep_ok")
        c_in = [sem(f"c_in{b}") for b in range(8)]
        c_z = sem("c_z")
        c_zg = sem("c_zg")
        c_cl = sem("c_cl")
        c_zb = sem("c_zb")
        c_x = sem("c_x")
        c_t_ps = sem("c_t_ps")
        c_t = sem("c_t")
        c_y_ps = sem("c_y_ps")
        c_y = sem("c_y")
        c_out = [sem(f"c_out{b}") for b in range(4)]

        class Slot:
            def __init__(self, g, k, fixed):
                self.g, self.k, self.fixed = g, k, fixed
                self.s = fixed if fixed is not None else g * GI + k

            def has(self, o):
                return self.fixed is None or 0 <= self.s + o < NI

            def before(self, o, n):
                return self.fixed is None or self.s + o >= n

            def img(self, o):
                return self.s + o

            def ring(self, o, n):
                return (self.k + o) % n

            def pair(self, o):
                return self.g * 2 + (self.k + o) // 2

            def has_group(self, o):
                return self.fixed is None or 0 <= self.g + o < NG

            def group_before(self, o, n):
                return self.fixed is None or self.g + o >= n

        def max_bank(n):
            if n == H - 1:
                return 1, n - 2
            return n % 3, (n - 3 if n >= 3 else (-4, -1, -2)[n])

        def wait_alone(eng, *waits):
            wait_all(eng, (begun, 1), *waits)

        def wait_all(eng, *waits):
            for _, value in waits:
                eng.compute_val(value)
            for sem, value in waits:
                eng.wait_ge(sem, value)

        class Seq:
            def __init__(self, eng, sem, per_group):
                self.eng, self.sem, self.per_group, self.base, self.n = eng, sem, per_group, 0, 0

            def mark(self, ins):
                ins.then_inc(self.sem, 1)
                self.n += 1
                return self.n

            def wait_mark(self, n):
                self.eng.wait_ge(self.sem, self.base + n)

            def wait_mark_alone(self, n):
                wait_alone(self.eng, (self.sem, self.base + n))

            def link(self, ins):
                self.wait_mark(self.mark(ins))

            def link_alone(self, ins):
                self.wait_mark_alone(self.mark(ins))

        def starting(t):
            return t.fixed is not None and t.g == 1 - GROUPS_AHEAD

        def haar_views(l):
            r, c = BAND[l]
            half = sd[:, :, 0:2 * r * c]
            rows = half.rearrange("p s (r two c) -> p s r two c", two=2, c=c)
            cur = (img[:] if l == 0 else coef[l - 1][:, 0].rearrange("p r c -> p (r c)"))
            return cur.rearrange("p (n two) -> p n two", two=2), half, rows[:, :, :, 0], rows[:, :, :, 1]

        def forward(eng, seq, l, stage=None):
            cur, half, even, odd = haar_views(l)
            if stage != 1:
                eng.tensor_tensor(half[:, 0], cur[:, :, 0], cur[:, :, 1], ALU.add)
                last = eng.tensor_tensor(half[:, 1], cur[:, :, 0], cur[:, :, 1], ALU.subtract)
                (seq.link if stage is None else seq.link_alone)(last)
            if stage == 0:
                return
            eng.tensor_tensor(coef[l][:, 0::2], even, odd, ALU.add)
            last = eng.tensor_tensor(coef[l][:, 1::2], even, odd, ALU.subtract)
            if l == 1:
                seq.link_alone(last)
            else:
                last.then_inc(fwd_done, 1)

        def inverse(eng, seq, l, stages=(0, 1, 2)):
            cur, half, even, odd = haar_views(l)
            if l == 0:
                cur = rec[:].rearrange("p (n two) -> p n two", two=2)
            if 0 in stages:
                eng.tensor_tensor(even, coef[l][:, 0::2], coef[l][:, 1::2], ALU.add)
            if 1 in stages:
                seq.link(eng.tensor_tensor(odd, coef[l][:, 0::2], coef[l][:, 1::2], ALU.subtract))
            if 2 not in stages:
                return
            eng.tensor_tensor(cur[:, :, 0], half[:, 0], half[:, 1], ALU.add)
            last = eng.tensor_tensor(cur[:, :, 1], half[:, 0], half[:, 1], ALU.subtract)
            if l:
                seq.link_alone(last)
            else:
                last.then_inc(rec_ok, 1)

        GROUPS_AHEAD = 2
        FIRST_SLOT = -GROUPS_AHEAD * GI
        LOOP = (1, NG - 2)

        def run(eng, slot, seq=None):
            for s in range(FIRST_SLOT, LOOP[0] * GI):
                slot(Slot(s // GI, s % GI, s))
            done = seq.n if seq else 0
            with eng.Fori(*LOOP) as g:
                if seq:
                    seq.n, seq.base = 0, (g - LOOP[0]) * seq.per_group + done
                for k in range(GI):
                    slot(Slot(g, k, None))
                if seq:
                    assert seq.n == seq.per_group, f"{seq.n} steps a group, not {seq.per_group}"
            if seq:
                seq.base, seq.n = 0, done + (LOOP[1] - LOOP[0]) * seq.per_group
            for s in range(LOOP[1] * GI, NI + 3):
                slot(Slot(s // GI, s % GI, s))

        BODY2 = 8

        def run2(eng, slot):
            for s in range(-6, BODY2):
                slot(Slot2(s // BODY2, s % BODY2, s))
            with eng.Fori(1, NI // BODY2 - 1) as g:
                for k in range(BODY2):
                    slot(Slot2(g, k, None))
            for s in range(NI - BODY2, NI + 2):
                slot(Slot2(s // BODY2, s % BODY2, s))

        class Slot2(Slot):
            def __init__(self, g, k, fixed):
                super().__init__(g, k, fixed)
                self.s = fixed if fixed is not None else g * BODY2 + k

            def turn(self, o, n):
                return self.g * (BODY2 // n) + (self.k + o) // n

        block = ctx.enter_context(nc.Block())

        NGATE = GI * 4 + 4
        NCONST = 4 + 3

        @block.sync
        def _(sp):
            sp.dma_start(img[:], x_v[0]).then_inc(x_in, 16)
            for i in range(GI):
                q = slice(i * IP, (i + 1) * IP)
                for l, w in enumerate((Wd3, Wd2, Wd1)):
                    sp.dma_start(gw[l][q].rearrange("p b f o -> p b (f o)"),
                                 w.rearrange("(b p f) o -> p b (f o)", b=3, p=IP)).then_inc(gates_in, 16)
                sp.dma_start(gwa[q], Wa.rearrange("(p f) o -> p (f o)", p=IP)).then_inc(gates_in, 16)
            for j, b in ((0, bd3), (3, bd2), (6, bd1), (9, ba)):
                sp.dma_start(gbias[:, j:j + b.shape[0]], b.partition_broadcast(P)).then_inc(gates_in, 16)
            for tile, w in ((h2[:, 0], Wq), (h2[:, 1], Wk), (wo[:], Wo), (wf[:], Wf)):
                sp.dma_start(tile, w.rearrange("(c p) n -> p c n", p=P)).then_inc(consts_in, 16)
            for row, b in ((bo_r, bo), (lng, ln_g), (lnb, ln_b)):
                sp.dma_start(row[:], b.partition_broadcast(P)).then_inc(consts_in, 16)

            def stack_half(t, o, f):
                b = t.ring(o, 2)
                waits = [(parts_out, 32 * (t.img(o) + 1))]
                if t.before(o, 2):
                    waits += [(sc_ps, H * t.img(o - 2) + HALF * (f + 1))]
                wait_all(sp, *waits)
                heads = slice(f * HALF, (f + 1) * HALF)
                for side, stack in enumerate((qs[b], ks[b])):
                    src = parts_dram[b, side, f]
                    part, row = P * T, HALF * T
                    if side == 0:
                        first = [[0, 2], [row, 2 * D], [1, row]]
                        last = [[2 * part, 2], [row, D], [1, row]]
                        start = 0
                    else:
                        first = [[part, 2], [row, 2 * D], [1, row]]
                        last = [[0, 2], [row, D], [1, row]]
                        start = 2 * part
                    rows = stack[:, heads].rearrange("p h t -> p (h t)")
                    sp.dma_start(rows[0:4 * D], bass.AP(tensor=src.tensor, offset=src.offset, ap=first)
                                 ).then_inc(stack_in[b][f], 16)
                    sp.dma_start(rows[4 * D:KS], bass.AP(tensor=src.tensor, offset=src.offset + start, ap=last)
                                 ).then_inc(stack_in[b][f], 16)

            def slot(t):
                if t.k == 0 and t.has_group(2) and t.group_before(2, 1):
                    sp.wait_ge(gprod, t.g + 2)
                    sp.dma_start(img[:], x_v[t.g + 2]).then_inc(x_in, 16)
                if t.has(1):
                    stack_half(t, 1, 1)
                if t.has_group(1):
                    waits = [(rec_ok, t.g + 2)]
                    if t.group_before(1, 1):
                        waits += [(xn_ok, t.s + 1), (bo_ok, t.s + 1)]
                    wait_all(sp, *waits)
                    sp.dma_start(h1[:, t.k].rearrange("p c e -> p (c e)"),
                                 rec[t.k * IP:(t.k + 1) * IP].rearrange("p (r n) -> p r n", n=QC * E)
                                 ).then_inc(h1_in[t.k], 16)
                if t.has(2):
                    b = t.ring(2, 2)
                    for n, side in enumerate((1, 0)):
                        waits = [(parts_ok, 2 * t.img(2) + n + 1)]
                        if n == 0 and t.before(2, 2):
                            waits += [(stack_in[b][1], STACK * (t.pair(0) + 1))]
                        wait_all(sp, *waits)
                        sp.dma_start(parts_dram[b, side].rearrange("f a p t -> p (f a) t"),
                                     parts[:, side].rearrange("p f a t -> p (f a) t")).then_inc(parts_out, 16)
                if t.has(2):
                    stack_half(t, 2, 0)
                if t.has(-1):
                    sp.wait_ge(h2_ok, t.img(0))
                    sp.dma_start(h2_dram[t.img(-1)], h2[:, t.ring(-1, 2)].rearrange("p c e -> p (c e)")
                                 ).then_inc(h2_out, 16)

            run(sp, slot)

            sp.wait_ge(h2_out, 16 * NI)
            sp.wait_ge(pv_ps, 4 * NI)

            def slot2(t):
                if t.has(6):
                    if t.before(6, 8):
                        sp.wait_ge(c_y, t.img(-1))
                    sp.dma_start(hh[t.ring(6, 8)], h2_dram[t.img(6)]).then_inc(c_in[t.ring(6, 8)], 16)
                if t.has(-1):
                    sp.wait_ge(c_y, t.img(0))
                    sp.dma_start(out_v[t.img(-1)], oy[t.ring(-1, 4)]).then_inc(c_out[t.ring(-1, 4)], 16)
            run2(sp, slot2)
            for b in range(4):
                sp.wait_ge(c_out[b], 16 * (NI // 4))

        @block.gpsimd
        def _(pool):
            seq = Seq(pool, pool_seq, POOL_STEPS)
            pool.memset(ident[:], 0.0).then_inc(begun, 1)
            pool.memset(minus_half[:], -0.5).then_inc(made, 1)
            pool.wait_ge(begun, 1)
            seq.link(pool.affine_select(out=ident[:], in_=ident[:], compare_op=ALU.not_equal, fill=1.0,
                                        base=0, pattern=[[-1, P]], channel_multiplier=1))
            for b in range(2):
                seq.link(pool.memset(ks[b][KS:P], 1.0))

            def slot(t):
                if t.has(-2):
                    waits = [(var2_ok, t.img(-1))]
                    if t.before(-2, 1):
                        waits += [(z_ok, t.img(-2)), (stat_ok, t.img(-2))]
                    wait_alone(pool, *waits)
                    var = mv2[:, :, 1]
                    seq.link(pool.tensor_scalar(rs2[:, 0], var, LN_EPS, None, ALU.add))
                    seq.link(pool.tensor_tensor(rs2[:, 1], rs2[:, 0], minus_half[:], ALU.pow))
                    seq.link(pool.tensor_tensor(rs2[:, 2], rs2[:, 1], rs2[:, 1], ALU.mult))
                    seq.link_alone(pool.tensor_tensor(rs2[:, 2], rs2[:, 2], var, ALU.mult))
                    seq.link(pool.tensor_scalar(rs2[:, 2], rs2[:, 2], FFN_LN_EPS, None, ALU.add))
                    seq.link(pool.tensor_tensor(rs2[:, 3], rs2[:, 2], minus_half[:], ALU.pow))
                    seq.link(pool.tensor_tensor(rs2[:, 4], rs2[:, 1], rs2[:, 3], ALU.mult))
                    seq.link_alone(pool.tensor_tensor(rs2[:, 2], rs2[:, 4], mv2[:, :, 0], ALU.mult))
                    pool.tensor_scalar(rs2[:, 2], rs2[:, 2], -1.0, None, ALU.mult).then_inc(rs2_ok, 1)
                if t.has(3):
                    wait_alone(pool, (var1_ok, t.img(3) + 1))
                    seq.link(pool.tensor_scalar(ve1[:], mv1[:, :, 1], LN_EPS, None, ALU.add))
                    pool.tensor_tensor(rstd1[:], ve1[:], minus_half[:], ALU.pow).then_inc(rstd1_ok, 1)
                if t.k == 3 and t.has_group(2) and t.group_before(2, 1):
                    pool.wait_ge(scaled, LEVELS * (t.g + 3))
                    inverse(pool, seq, 0, (0,))
                if t.has(2):
                    for n, side in enumerate((1, 0)):
                        pool.wait_ge(mid_ok, 2 * t.img(2) + n + 1)
                        if n == 0 and t.before(2, 1):
                            pool.wait_ge(parts_out, 32 * t.img(2))
                        _, middle_, low = PART[side]
                        pool.tensor_tensor(parts[:, side, :, low], qkr[:, side], parts[:, side, :, middle_],
                                           ALU.subtract).then_inc(parts_ok, 1)
                if t.has(-2):
                    pool.wait_ge(z_ok, t.img(-1))
                    seq.link(pool.tensor_tensor(z[:], z[:], lng_v, ALU.mult))
                    pool.tensor_tensor(z[:], z[:], lnb_v, ALU.add).then_inc(zb_ok, 1)
                if t.has(2):
                    pool.wait_ge(xn_ok, t.img(2) + 1)
                    if t.before(2, GI):
                        pool.wait_ge(h2_ok, t.img(-1))
                    pool.tensor_tensor(h1b[:, t.ring(2, GI)], h1[:, t.ring(2, GI)], bo_v, ALU.add).then_inc(bo_ok, 1)
                if t.k == 0 and t.has_group(2) and t.group_before(2, 1):
                    pool.wait_ge(x_in, 16 * (t.g + 3))
                    pool.wait_ge(rec_ok, t.g + 2)
                    forward(pool, seq, 0, 0)
                    if not starting(t):
                        forward(pool, seq, 0, 1)
                if t.k == 1 and starting(t):
                    forward(pool, seq, 0, 1)
                if t.k == 1 and t.has_group(2) and t.group_before(2, 1):
                    pool.wait_ge(fwd_done, 2 * (t.g + 3) - 1)
                    forward(pool, seq, 1)
                    forward(pool, seq, 2)
                if t.k == 2 and t.has_group(2) and t.group_before(2, 1):
                    pool.wait_ge(scaled, LEVELS * (t.g + 3) - 2)
                    inverse(pool, seq, 2)
                    pool.wait_ge(scaled, LEVELS * (t.g + 3) - 1)
                    inverse(pool, seq, 1)
                if t.k == 3 and t.has_group(2) and t.group_before(2, 1):
                    pool.wait_ge(h1_in[GI - 1], H1_IN * (t.g + 2))
                    inverse(pool, seq, 0, (1, 2))

            pool.memset(vaug[:, :, :, :, D:2 * D], 1.0).then_inc(made, 1)
            pool.wait_ge(consts_in, 16 * NCONST)
            run(pool, slot, seq)

            def slot2(t):
                if t.has(3):
                    pool.wait_ge(c_zg, t.img(3) + 1)
                    z_ = zz[t.ring(3, GI)].rearrange("p (c e) -> p c e", c=QC)
                    pool.tensor_tensor(z_, z_, lnb_v, ALU.add).then_inc(c_zb, 1)
            run2(pool, slot2)

        @block.scalar
        def _(act):
            def copy(out, in_, scale=1.0):
                return act.activation(out, in_, ACT.Copy, scale=scale)

            def max_high(t, o, half):
                act.wait_ge(mT_ps, 2 * t.img(o) + half + 1)
                if t.before(o, 1):
                    act.wait_ge(mrow_in[t.ring(o - 1, 2)], MROW * (t.pair(o - 1) + 1))
                if half or t.before(o, 1):
                    act.wait_ge(mlo_ok, 2 * t.img(o) + half)
                copy(m32[:], ps_b[0:HC, 0:T])
                copy(mT[:, half, 0], ps_b[0:HC, 0:T]).then_inc(mhi_ok, 1)

            def max_rows(t, o, half):
                act.wait_ge(mlo_ok, 2 * t.img(o) + half + 1)
                for part in range(2):
                    act.dma_start(qs[t.ring(o, 2)][KS + part:KS + part + 1, half * HC:(half + 1) * HC],
                                 mT[:, half, part]).then_inc(mrow_in[t.ring(o, 2)], 16)

            def evac_qk(t, side, ps, ready, done, scale):
                act.wait_ge(ready, t.img(2) + 1)
                if t.before(2, 1):
                    act.wait_ge(res_ok, 2 * t.img(2))
                    act.wait_ge(v_ps, t.img(2))
                    act.wait_ge(parts_out, 32 * t.img(2))
                copy(qk[:, side].rearrange("p c t -> p (c t)"), ps[:], scale)
                copy(parts[:, side, :, PART[side][0]], ps[:].rearrange("p (c t) -> p c t", c=EC),
                     scale).then_inc(done, 1)

            def middle(t, n, side):
                act.wait_ge(res_ok, 2 * t.img(2) + n + 1)
                copy(parts[:, side, :, PART[side][1]], qkr[:, side]).then_inc(mid_ok, 1)

            def evac_oT(t, o, quad):
                act.wait_ge(pv_ps, 4 * t.img(o) + quad + 1)
                if t.before(o, 1):
                    act.wait_ge(o1_ps, 2 * t.img(o - 1) + quad // 2 + 1)
                copy(oT[:, quad], ps_o[:, 0:T]).then_inc(oT_ok, 1)

            def slot(t):
                for h in range(H):
                    if t.has(0):
                        act.wait_ge(sc_ps, H * t.img(0) + h + 1)
                        if h >= 8 or t.before(0, 1):
                            act.wait_ge(pv_ps, 4 * t.img(0) + h // 4 - 1)
                        act.activation(prob[:, h % 8].rearrange("p c t -> p (c t)"), ps_s[h % 2][:],
                                       ACT.Exp).then_inc(exp_ok, 1)
                    if h == 0 and t.has(2):
                        act.wait_ge(xnT_ps, t.img(2) + 1)
                        if t.before(2, 1):
                            act.wait_ge(qT_ps, t.img(2))
                        copy(xnT[:].rearrange("p c t -> p (c t)"), ps_a[:]).then_inc(xnT_ok, 1)
                    if h == 1 and t.has(0):
                        max_high(t, 0, 1)
                    if h == 2 and t.has(2):
                        evac_qk(t, 1, ps_a, kT_ps, kT_ok, 1.0)
                    if h == 3 and t.has(-1):
                        evac_oT(t, -1, 3)
                    if h == 3 and t.has(2):
                        evac_qk(t, 0, ps_b, qT_ps, qT_ok, SCALE)
                    if h == 4 and t.has(2):
                        middle(t, 0, 1)
                    if h == 4 and t.has(0):
                        max_rows(t, 0, 1)
                    if h == 12 and t.has(1):
                        max_rows(t, 1, 0)
                    if h == 5 and t.has(2):
                        middle(t, 1, 0)
                        act.wait_ge(v_ps, t.img(2) + 1)
                        if t.before(2, GI):
                            act.wait_ge(pv_ps, 4 * t.img(-1))
                        for c in range(QC):
                            last = copy(vaug[:, t.ring(2, GI), c, :, 0:D].rearrange("p (f h) d -> p f h d", f=EC),
                                        ps_a[:, c * E:(c + 1) * E].rearrange("p (f d h) -> p f h d", f=EC, d=D))
                        last.then_inc(v_ok, 1)
                    if h in (7, 8) and t.has(-2):
                        c = h - 7
                        act.wait_ge(rs2_ok, t.img(-1))
                        if c == 0 and t.before(-2, 1):
                            act.wait_ge(zmax_ok, t.img(-2))
                        last = act.activation(z[:, c], h2[:, t.ring(-2, 2), c], ACT.Identity,
                                              bias=rs2[:, 2, c:c + 1], scale=rs2[:, 4, c:c + 1])
                        if c == QC - 1:
                            last.then_inc(z_ok, 1)
                    if h == 9 and t.has(1):
                        max_high(t, 1, 0)
                    if h in (7, 11, 15) and t.has(0):
                        evac_oT(t, 0, (h - 7) // 4)
                    if h == 10 and t.has(-1):
                        act.wait_ge(attT_ps, t.img(0))
                        if t.before(-1, 1):
                            act.wait_ge(proj_ps, t.img(-1))
                        copy(attT[:].rearrange("p c t -> p (c t)"), ps_a[:]).then_inc(attT_ok, 1)
                    if h == 11 and t.k == 2 and t.has_group(2):
                        act.wait_ge(glog_ok, t.g + 3)
                        act.activation(gexp[:], glog[:], ACT.Exp).then_inc(gexp_ok, 1)
                    if (t.k, h) in SCALE_STEPS and t.has_group(2):
                        l, bands = SCALE_STEPS[(t.k, h)]
                        if l == LEVELS - 1:
                            act.wait_ge(gate_ok, t.g + 3)
                            copy(coef[l][:, 0], coef[l][:, 0], gate[:, 9:10])
                        for band in bands:
                            last = copy(coef[l][:, 1 + band], coef[l][:, 1 + band],
                                        gate[:, 3 * l + band:3 * l + band + 1])
                        if bands[-1] == 2:
                            last.then_inc(scaled, 1)

            run(act, slot)

            def slot2(t):
                if t.has(1):
                    act.wait_ge(c_t_ps, t.img(1) + 1)
                    if t.before(1, 2):
                        act.wait_ge(c_y_ps, t.img(0))
                    copy(xT[t.ring(1, 2)], ps_s[t.ring(1, 2)][:]).then_inc(c_t, 1)
                if t.has(4):
                    i, b = t.img(4), t.ring(4, GI)
                    if t.before(4, GI):
                        act.wait_ge(c_t_ps, t.img(1))
                    if not t.before(4, 1):
                        act.wait_ge(stat_ok, NI)
                    act.wait_ge(c_in[t.ring(4, 8)], 16 * (t.turn(4, 8) + 1))
                    for c in range(QC):
                        e = slice(c * E, (c + 1) * E)
                        last = act.activation(zz[b][:, e], hh[t.ring(4, 8)][:, e], ACT.Identity,
                                              bias=stats[:, i, 0, c:c + 1], scale=stats[:, i, 1, c:c + 1])
                    last.then_inc(c_z, 1)
            run2(act, slot2)

        @block.vector
        def _(dve):
            seq = Seq(dve, dve_seq, DVE_STEPS)
            link = seq.link
            dve.memset(ones[:], 1.0).then_inc(made, 1)
            link(dve.memset(blk1[:], 0.0))
            for i in range(GI):
                dve.memset(blk1[i * IP:(i + 1) * IP, i * IP:(i + 1) * IP], 1.0).then_inc(made, 1)
            dve.memset(zmax[:], 0.0).then_inc(made, 1)
            dve.memset(gpart[:], 0.0).then_inc(made, 1)

            def order_weights():
                dve.wait_ge(consts_in, 16 * NCONST)
                for side, w in enumerate((wq, wk)):
                    dve.tensor_copy(w[:].rearrange("p e (f d h) -> p (e f) d h", f=EC, d=D),
                                    h2[:, side].rearrange("p e (f h d) -> p (e f) d h", f=EC, d=D)).then_inc(w_ok, 1)

            def ternary():
                link(dve.tensor_reduce(fs[:, 0:1], wf[:].rearrange("p c n -> p (c n)"), AX.X, ALU.add,
                                       apply_absolute_value=True))
                dve.nop().then_inc(prep_ok, 1)
                dve.wait_ge(prep_ps, 1)
                dve.tensor_scalar(fs[:, 1:2], ps_a[:, 0:1], 1.0 / (E * E), None, ALU.mult).then_inc(mean_ok, 1)
                dve.wait_ge(mean_ok, 1)
                link(dve.tensor_scalar(fs[:, 2:3], fs[:, 1:2], FFN_EPS, None, ALU.add))
                link(dve.reciprocal(fs[:, 3:4], fs[:, 2:3]))
                link(dve.tensor_scalar(wf[:], wf[:], fs[:, 3:4], 1.0, ALU.mult, ALU.min))
                link(dve.tensor_scalar(wf[:], wf[:], -1.0, ROUND, ALU.max, ALU.add))
                link(dve.tensor_scalar(wf[:], wf[:], -ROUND, None, ALU.add))

            def gate_product(n):
                half, column = (n % 2, n // 2) if n < 6 else (0, n - 3)
                l, o = divmod(column, 3)
                if l < LEVELS:
                    data = coef[l][:, 1:4].rearrange("p b r c -> p (b r c)")
                    w = gw[l][:].rearrange("p b f o -> p (b f) o")[:, :, o]
                else:
                    data, w = coef[LEVELS - 1][:, 0].rearrange("p r c -> p (r c)"), gwa[:]
                size = data.shape[1] // (2 if n < 6 else 1)
                part = slice(half * size, (half + 1) * size)
                return dve.tensor_tensor_reduce(out=img[:, 0:size], in0=data[:, part], in1=w[:, part], scale=1.0,
                                                scalar=0.0, op0=ALU.mult, op1=ALU.add,
                                                accum_out=gpart[:, half, column:column + 1])

            def gate_logits():
                for l in range(LEVELS):
                    q = slice(3 * l, 3 * l + 3 + (l == LEVELS - 1))
                    last = dve.scalar_tensor_tensor(glog[:, q], ps_b[:, T + q.start:T + q.stop], 0.5 ** (l + 1),
                                                    gbias[:, q], ALU.mult, ALU.add)
                link(last)
                v = glog[:, 0:9].rearrange("p (l b) -> p l b", b=3)
                link(dve.tensor_reduce(gmx[:], v, AX.X, ALU.max))
                dve.tensor_tensor(v, v, gmx[:].unsqueeze(2).to_broadcast([P, 3, 3]), ALU.subtract)
                dve.tensor_scalar(glog[:, 9:10], glog[:, 9:10], -1.0, None, ALU.mult).then_inc(glog_ok, 1)

            def gate_values(g3):
                dve.wait_ge(gexp_ok, g3)
                v = gexp[:, 0:9].rearrange("p (l b) -> p l b", b=3)
                dve.tensor_reduce(gsum[:, 0:3], v, AX.X, ALU.add)
                link(dve.tensor_scalar(gsum[:, 3:4], gexp[:, 9:10], 1.0, None, ALU.add))
                link(dve.reciprocal(grec[:], gsum[:]))
                for l in range(LEVELS):
                    dve.tensor_scalar(gate[:, 3 * l:3 * l + 3], gexp[:, 3 * l:3 * l + 3], grec[:, l:l + 1],
                                      0.25 ** (l + 1), ALU.mult, ALU.mult)
                dve.tensor_scalar(gate[:, 9:10], grec[:, 3:4], 0.25 ** LEVELS, None, ALU.mult).then_inc(gate_ok, 1)

            def max_low(t, o, half):
                dve.wait_ge(mhi_ok, 2 * t.img(o) + half + 1)
                dve.tensor_tensor(mT[:, half, 1], m32[:], mT[:, half, 0], ALU.subtract).then_inc(mlo_ok, 1)

            def piece(t, o, n):
                pair, c = divmod(n, QC)
                half, j = divmod(pair, 4)
                dve.wait_ge(msc_ps, H * t.img(o) + n + 1)
                if n % 8 == 0 and t.before(o, 1):
                    dve.wait_ge(mT_ps, 2 * t.img(o - 1) + half + 1)
                scores = ps_m[max_bank(n)[0]][:].rearrange("p (j t) -> p j t", j=2)
                dve.tensor_reduce(negm[:, half, c, 2 * j:2 * j + 2], scores, AX.X, ALU.max, negate=True).then_inc(max_ok, 1)

            def reciprocals(t, bank, ps):
                v = ps[:].rearrange("p (qc j w) -> p qc j w", j=4, w=2 * D)
                dve.wait_ge(o1_ps, 2 * t.img(-1) + bank + 1)
                return seq.mark(dve.reciprocal(rden[:, bank].rearrange("p q c j -> p (q c) j"), v[:, :, :, D]))

            def normalise(t, bank, ps, inverted):
                v = ps[:].rearrange("p (qc j w) -> p qc j w", j=4, w=2 * D)
                seq.wait_mark(inverted)
                if bank == 0 and t.before(-1, 1):
                    dve.wait_ge(attT_ps, t.img(-1))
                v5 = v.rearrange("p (q c) j w -> p q c j w", c=QC)
                for c in range(QC):
                    last = dve.tensor_tensor(
                        att[:, c, bank * P:(bank + 1) * P].rearrange("p (q j d) -> p q j d", q=2, j=4),
                        v5[:, :, c, :, 0:D], rden[:, bank, :, c].unsqueeze(3).to_broadcast([P, 2, 4, D]), ALU.mult)
                last.then_inc(att_ok, 1)

            product = None

            def slot(t):
                nonlocal product
                if t.fixed == FIRST_SLOT:
                    dve.wait_ge(x_in, 16)
                    for l in range(LEVELS):
                        if l == 1:
                            dve.wait_ge(fwd_done, 1)
                        forward(dve, seq, l)
                if t.fixed == FIRST_SLOT + 3:
                    order_weights()
                    for l in reversed(range(LEVELS)):
                        dve.wait_ge(scaled, LEVELS - l)
                        inverse(dve, seq, l)
                for h in range(H):
                    if h == 11 and t.k == 2 and t.has_group(2):
                        dve.wait_ge(glog_ps, t.g + 3)
                        gate_logits()
                    if h in (7, 8) and t.has(-1):
                        inverted = reciprocals(t, h - 7, ps_b if h == 7 else ps_a)
                    if h == 1 and t.has(-2):
                        dve.wait_ge(h2_ok, t.img(-1))
                        for c in range(QC):
                            last = dve.bn_stats(bn2[:, c], h2[:, t.ring(-2, 2), c])
                        taken = seq.mark(last)
                    if h == 2 and t.has(3):
                        dve.wait_ge(h1_in[t.ring(3, GI)], H1_IN * ((t.g + (t.k + 3) // GI) + 1))
                        for c in range(QC):
                            last = dve.bn_stats(bn1[:, c], h1[:, t.ring(3, GI), c])
                        taken = seq.mark(last)
                    if h == 0 and t.has(0):
                        piece(t, 0, H - 1)
                    if h >= 1 and t.has(1):
                        piece(t, 1, h - 1)
                    if h == 1 and t.has(-2):
                        waits = [(rs2_ok, t.img(-2))] if t.before(-2, 1) else []
                        wait_alone(dve, *waits, (seq.sem, seq.base + taken))
                        for c in range(QC):
                            last = dve.bn_aggr(mv2[:, c], bn2[:, c])
                        last.then_inc(var2_ok, 1)
                    if h == 2 and t.has(3):
                        waits = [(rstd1_ok, t.img(3))] if t.before(3, 1) else []
                        wait_alone(dve, *waits, (seq.sem, seq.base + taken))
                        for c in range(QC):
                            last = dve.bn_aggr(mv1[:, c], bn1[:, c])
                        last.then_inc(var1_ok, 1)
                    if h == 2 and t.has(0):
                        max_low(t, 0, 1)
                    if h == 5 and t.has(-2):
                        dve.wait_ge(rs2_ok, t.img(-1))
                        dve.tensor_copy(stats[:, t.img(-2), 0], rs2[:, 2])
                        dve.tensor_copy(stats[:, t.img(-2), 1], rs2[:, 4]).then_inc(stat_ok, 1)
                    if h in (3, 4) and t.has(2):
                        side = 4 - h
                        dve.wait_ge(kT_ok if side else qT_ok, t.img(2) + 1)
                        if h == 3 and t.before(2, 1):
                            dve.wait_ge(parts_ok, 2 * t.img(2))
                        dve.tensor_tensor(qkr[:, side], qk[:, side], parts[:, side, :, PART[side][0]],
                                          ALU.subtract).then_inc(res_ok, 1)
                    if h == 3 and t.has(-3):
                        dve.wait_ge(zb_ok, t.img(-2))
                        if t.before(-3, 1):
                            dve.wait_ge(zmax_ok, t.img(-3))
                        b = t.ring(-3, 2)
                        dve.tensor_tensor(zmax[:, 2:3], zmax[:, 2:3], zmax[:, 1 - b:2 - b], ALU.max)
                        dve.tensor_reduce(zmax[:, b:b + 1], z[:].rearrange("p c e -> p (c e)"), AX.X, ALU.max,
                                          apply_absolute_value=True).then_inc(zmax_ok, 1)
                    if t.has_group(2):
                        if t.fixed == FIRST_SLOT + GI + 1 and h == 3:
                            ternary()
                        for n in (FIRST_GATE_STEPS if starting(t) else GATE_STEPS).get((t.k, h), ()):
                            if n == 0 and t.fixed is not None and t.g == -GROUPS_AHEAD:
                                dve.wait_ge(gates_in, 16 * NGATE)
                            if n == 0:
                                dve.wait_ge(fwd_done, 2 * (t.g + 3) - 1)
                            if n == 6:
                                dve.wait_ge(fwd_done, 2 * (t.g + 3))
                            if n > 0:
                                seq.wait_mark(product)
                            if n == 12:
                                gate_product(n).then_inc(gprod, 1)
                            else:
                                product = seq.mark(gate_product(n))
                    if h in (7, 8) and t.has(-1):
                        normalise(t, h - 7, ps_b if h == 7 else ps_a, inverted)
                    if h == 10 and t.has(1):
                        max_low(t, 1, 0)
                    if h == 6 and t.has(3):
                        dve.wait_ge(rstd1_ok, t.img(3) + 1)
                        if t.before(3, 2):
                            dve.wait_ge(xnT_ps, t.img(2))
                        for c in range(QC):
                            last = dve.tensor_scalar(xn[:, t.ring(3, 2), c], h1[:, t.ring(3, GI), c],
                                                     mv1[:, c, 0:1], rstd1[:, c:c + 1], ALU.subtract, ALU.mult)
                        last.then_inc(xn_ok, 1)
                    if h == 15 and t.has(-1):
                        b = t.ring(-1, 2)
                        dve.wait_ge(proj_ps, t.img(0))
                        dve.wait_ge(bo_ok, t.img(0))
                        if t.before(-1, 2):
                            dve.wait_ge(h2_out, 16 * t.img(-1))
                        dve.tensor_tensor(h2[:, b].rearrange("p c e -> p (c e)"), ps_b[:],
                                          h1b[:, t.ring(-1, GI)].rearrange("p c e -> p (c e)"), ALU.add).then_inc(h2_ok, 1)
                    if h == 12 and t.k == 2 and t.has_group(2):
                        gate_values(t.g + 3)

            run(dve, slot, seq)

            def factors():
                dve.wait_ge(zmax_ok, NI)
                dve.tensor_tensor(zmax[:, 2:3], zmax[:, 2:3], zmax[:, (NI - 1) % 2:(NI - 1) % 2 + 1],
                                  ALU.max).then_inc(prep_ok, 1)
                dve.wait_ge(prep_ps, 2)
                link(dve.tensor_reduce(zrow[:, 0:1], ps_a[0:1, 0:P], AX.X, ALU.max))
                dve.nop().then_inc(prep_ok, 1)
                dve.wait_ge(prep_ps, 3)
                link(dve.tensor_scalar(fs[:, 4:5], ps_b[:, 0:1], 1.0, None, ALU.mult))
                link(dve.reciprocal(fs[:, 5:6], fs[:, 4:5]))
                link(dve.tensor_scalar(fs[:, 5:6], fs[:, 5:6], QB, None, ALU.mult))
                link(dve.tensor_scalar(fs[:, 6:7], fs[:, 4:5], fs[:, 1:2], 1.0 / QB, ALU.mult, ALU.mult))

            def slot2(t):
                if t.fixed == -2:
                    factors()
                if t.has(-1):
                    b = t.ring(-1, 2)
                    dve.wait_ge(c_y_ps, t.img(0))
                    if t.before(-1, GI):
                        dve.wait_ge(c_out[t.ring(-1, 4)], 16 * t.turn(-1, 4))
                    dve.scalar_tensor_tensor(oy[t.ring(-1, 4)], ps_m[b][:], fs[:, 6:7], hh[t.ring(-1, 8)],
                                             ALU.mult, ALU.add).then_inc(c_y, 1)
                if t.has(3):
                    b = t.ring(3, GI)
                    dve.wait_ge(c_z, t.img(3) + 1)
                    z_ = zz[b].rearrange("p (c e) -> p c e", c=QC)
                    dve.tensor_tensor(z_, z_, lng_v, ALU.mult).then_inc(c_zg, 1)
                if t.has(2):
                    b = t.ring(2, GI)
                    dve.wait_ge(c_zb, t.img(2) + 1)
                    dve.tensor_scalar(zz[b], zz[b], fs[:, 5:6], CLIP, ALU.mult, ALU.min).then_inc(c_cl, 1)
                    dve.wait_ge(c_cl, t.img(2) + 1)
                    dve.tensor_scalar(zz[b], zz[b], -CLIP, None, ALU.max).then_inc(c_x, 1)
            run2(dve, slot2)

        @block.tensor
        def _(pe):
            def transposes(t, ps, tile):
                for e in range(2):
                    for c in range(2):
                        last = pe.transpose(ps[:, e * T + c * P:e * T + (c + 1) * P], tile[:, c, e * P:(e + 1) * P],
                                            ident[:])
                return last

            def project(ps, w):
                for f in range(EC):
                    for e in range(EC):
                        last = pe.matmul(ps[:, f * T:(f + 1) * T],
                                         w[:, e, f * P:(f + 1) * P], xnT[:, e], start=(e == 0), stop=(e == EC - 1))
                return last

            def maxima_rows(t, o, half):
                pe.wait_ge(max_ok, H * t.img(o) + 8 * (half + 1))
                for c in range(QC):
                    last = pe.transpose(ps_b[0:HC, c * P:(c + 1) * P], negm[:, half, c], ident[:])
                last.then_inc(mT_ps, 1)

            def piece(t, o, n):
                pair, c = divmod(n, QC)
                if n % HALF == 0:
                    pe.wait_ge(stack_in[t.ring(o, 2)][n // HALF], STACK * (t.pair(o) + 1))
                bank, last_use = max_bank(n)
                if last_use >= 0 or t.before(o, 1):
                    pe.wait_ge(max_ok, H * t.img(o) + last_use + 1)
                for j in range(2):
                    q = qs[t.ring(o, 2)][0:KS, 2 * pair + j, c * P:(c + 1) * P]
                    last = pe.matmul(ps_m[bank][:, j * T:(j + 1) * T], q, ks[t.ring(o, 2)][0:KS, 2 * pair + j],
                                     start=True, stop=True)
                last.then_inc(msc_ps, 1)

            def values(t, o, quad):
                if quad == 0:
                    pe.wait_ge(v_ok, t.img(o) + 1)
                pe.wait_ge(exp_ok, H * t.img(o) + 4 * (quad + 1))
                if quad or t.before(o, 1):
                    pe.wait_ge(oT_ok, 4 * t.img(o) + quad)
                for c in range(QC):
                    for j in range(4):
                        last = pe.matmul(ps_o[j * 2 * D:(j + 1) * 2 * D, 0:T],
                                         vaug[:, t.ring(o, GI), c, 4 * quad + j], prob[:, (4 * quad + j) % 8, c],
                                         start=(c == 0), stop=(c == QC - 1))
                last.then_inc(pv_ps, 1)

            def tokens(t, bank, ps):
                pe.wait_ge(oT_ok, 4 * t.img(-1) + 2 * bank + 2)
                for q in range(2):
                    for c in range(QC):
                        last = pe.transpose(ps[:, (q * QC + c) * P:(q * QC + c + 1) * P],
                                            oT[:, 2 * bank + q, c * P:(c + 1) * P], ident[:])
                last.then_inc(o1_ps, 1)

            def slot(t):
                if t.fixed == FIRST_SLOT + GI + 1:
                    pe.wait_ge(prep_ok, 1)
                    pe.matmul(ps_a[:, 0:1], ones[:], fs[:, 0:1], start=True, stop=True).then_inc(prep_ps, 1)
                for h in range(H):
                    if t.has(0):
                        if h % HC == 0:
                            pe.wait_ge(mrow_in[t.ring(0, 2)], MROW * t.pair(0) + 32 * (h // HC + 1))
                        if h >= 2 or t.before(0, 1):
                            pe.wait_ge(exp_ok, H * t.img(0) + h - 1)
                        for c in range(QC):
                            last = pe.matmul(ps_s[h % 2][:, c * T:(c + 1) * T],
                                             ks[t.ring(0, 2)][0:KM, h, c * P:(c + 1) * P], qs[t.ring(0, 2)][0:KM, h],
                                             start=True, stop=True)
                        last.then_inc(sc_ps, 1)
                    if h == 0 and t.has(0):
                        piece(t, 0, H - 1)
                    if h >= 1 and t.has(1):
                        piece(t, 1, h - 1)
                    if h == 1 and t.has(-1):
                        values(t, -1, 3)
                    if h in (5, 9, 13) and t.has(0):
                        values(t, 0, (h - 5) // 4)
                    if h == 0 and t.has(2):
                        if t.has(-2):
                            pe.wait_ge(attT_ok, t.img(-1))
                        elif t.has(1):
                            pe.wait_ge(v_ok, t.img(2))
                        else:
                            pe.wait_ge(mean_ok, 1)
                        pe.wait_ge(xn_ok, t.img(2) + 1)
                        transposes(t, ps_a, xn[:, t.ring(2, 2)]).then_inc(xnT_ps, 1)
                    if h == 1 and t.has(0):
                        if t.has(-2):
                            pe.wait_ge(h2_ok, t.img(-1))
                        else:
                            pe.wait_ge(mhi_ok, 2 * t.img(0) + 1)
                        maxima_rows(t, 0, 1)
                    if h == 2 and t.has(2):
                        if not t.before(2, 1):
                            pe.wait_ge(w_ok, 2)
                        pe.wait_ge(xnT_ok, t.img(2) + 1)
                        project(ps_a, wk).then_inc(kT_ps, 1)
                    if h == 3 and t.has(2):
                        if t.has(0):
                            pe.wait_ge(mhi_ok, 2 * t.img(0) + 2)
                        elif t.has(1):
                            pe.wait_ge(qT_ok, t.img(2))
                        project(ps_b, wq).then_inc(qT_ps, 1)
                    if h == 5 and t.has(2):
                        pe.wait_ge(kT_ok, t.img(2) + 1)
                        transposes_kT(t)
                    if h == 6 and t.has(-1):
                        if t.has(2):
                            pe.wait_ge(qT_ok, t.img(2) + 1)
                        elif t.has(0):
                            pe.wait_ge(mhi_ok, 2 * t.img(0) + 2)
                        else:
                            pe.wait_ge(h2_ok, t.img(-1))
                        tokens(t, 0, ps_b)
                    if h == 7 and t.has(-1):
                        if t.has(2):
                            pe.wait_ge(v_ok, t.img(2) + 1)
                        else:
                            pe.wait_ge(attT_ok, t.img(-1))
                        tokens(t, 1, ps_a)
                    if h == 9 and t.has(1):
                        if t.has(-1):
                            pe.wait_ge(att_ok, 2 * t.img(-1) + 1)
                        else:
                            pe.wait_ge(qT_ok, t.img(2) + 1)
                        maxima_rows(t, 1, 0)
                    if h == 10 and t.has(-1):
                        pe.wait_ge(att_ok, 2 * t.img(0))
                        transposes(t, ps_a, att).then_inc(attT_ps, 1)
                    if h == (13 if t.k == 2 else 12) and t.has(-1):
                        pe.wait_ge(attT_ok, t.img(0))
                        if t.has(1):
                            pe.wait_ge(mhi_ok, 2 * t.img(1) + 1)
                        if t.k == 2 and t.has_group(2):
                            pe.wait_ge(glog_ok, t.g + 3)
                        project_out(0)
                    if h == 14 and t.has(-1):
                        project_out(1).then_inc(proj_ps, 1)
                    if h == 10 and t.k == 2 and t.has_group(2):
                        pe.wait_ge(gprod, t.g + 3)
                        if t.has(1):
                            pe.wait_ge(mhi_ok, 2 * t.img(1) + 1)
                        for half in range(2):
                            last = pe.matmul(ps_b[:, T:T + 10], blk1[:], gpart[:, half], start=(half == 0),
                                             stop=(half == 1))
                        last.then_inc(glog_ps, 1)

            def project_out(c):
                for e in range(EC):
                    last = pe.matmul(ps_b[:, c * E:(c + 1) * E], attT[:, e, c * P:(c + 1) * P], wo[:, e],
                                     start=(e == 0), stop=(e == EC - 1))
                return last

            def transposes_kT(t):
                for c in range(QC):
                    for f in range(EC):
                        last = pe.transpose(ps_a[:, (c * EC + f) * P:(c * EC + f + 1) * P],
                                            qk[:, 1, f, c * P:(c + 1) * P], ident[:])
                last.then_inc(v_ps, 1)

            pe.wait_ge(made, MADE)
            pe.wait_ge(consts_in, 16 * NCONST)
            run(pe, slot)
            pe.wait_ge(prep_ok, 2)
            pe.transpose(ps_a[0:1, 0:P], zmax[:, 2:3], ident[:]).then_inc(prep_ps, 1)
            pe.wait_ge(prep_ok, 3)
            pe.matmul(ps_b[:, 0:1], ones[0:1, :], zrow[:, 0:1], start=True, stop=True).then_inc(prep_ps, 1)

            def slot2(t):
                if t.has(1):
                    b = t.ring(1, 2)
                    pe.wait_ge(c_x, t.img(1) + 1)
                    if t.before(1, 2):
                        pe.wait_ge(c_t, t.img(0))
                    x_ = zz[t.ring(1, GI)].rearrange("p (c e) -> p c e", c=QC)
                    transposes(t, ps_s[b], x_).then_inc(c_t_ps, 1)
                if t.has(0):
                    b = t.ring(0, 2)
                    pe.wait_ge(c_t, t.img(0) + 1)
                    if t.before(0, 2):
                        pe.wait_ge(c_y, t.img(-1))
                    for c in range(QC):
                        for e in range(EC):
                            last = pe.matmul(ps_m[b][:, c * E:(c + 1) * E],
                                             xT[b][:, e * T + c * P:e * T + (c + 1) * P],
                                             wf[:, e], start=(e == 0), stop=(e == EC - 1))
                    last.then_inc(c_y_ps, 1)
            run2(pe, slot2)


_INS = ["x", "L0_tok_Wa", "L0_tok_ba", "L0_tok_Wd1", "L0_tok_bd1", "L0_tok_Wd2", "L0_tok_bd2", "L0_tok_Wd3",
        "L0_tok_bd3", "L0_attn_Wk", "L0_attn_Wq", "L0_attn_Wo", "L0_attn_bo", "L0_ffn_weight", "L0_ffn_ln_gamma",
        "L0_ffn_ln_beta"]


def kernel(**inputs):
    import numpy as np
    import concourse.bacc as bacc
    from concourse.bass_utils import run_bass_kernel_spmd

    nc = bacc.Bacc("TRN2", target_bir_lowering=False, num_devices=1)
    arrays, args = {}, []
    for name in _INS:
        a = np.ascontiguousarray(inputs[name])
        arrays[name] = a
        args.append(nc.dram_tensor(name, a.shape, mybir.dt.from_np(a.dtype), kind="ExternalInput").ap())
    out = nc.dram_tensor("out", (NI, T, E), F32, kind="ExternalOutput").ap()
    build(nc, *args, out)
    return run_bass_kernel_spmd(nc, [arrays], core_ids=[0]).results[0]["out"]
```
